# Optimizing a Trainium2 kernel written in Bass

```python
import numpy as np
import jax
import jax.numpy as jnp

def _softmax(x, axis=-1):
    return jax.nn.softmax(x, axis=axis)

def _gelu(x):
    return jax.nn.gelu(x, approximate=True)

def _silu(x):
    return jax.nn.silu(x)

def _sigmoid(x):
    return jax.nn.sigmoid(x)

def _layernorm(x, axis=-1, eps=1e-05):
    m = jnp.mean(x, axis=axis, keepdims=True)
    v = jnp.var(x, axis=axis, keepdims=True)
    return (x - m) / jnp.sqrt(v + eps)

def _scatter_add(tgt, idx, src, axis=0):
    return tgt.at[idx].add(src)

def _segment_sum(src, seg, n):
    return jax.ops.segment_sum(src, seg, n)
kernel_name = 'mk_prb_d1_jaxref_r2_e63069'

def setup_inputs(seed: int=0):
    np.random.seed(seed)
    _w = jnp.asarray

    def _L0_attn_setup():
        import jax, jax.numpy as jnp
        import numpy as np
        B, N, DM, H = (1, 1024, 512, 16)
        CURV = 1.0
        key = jax.random.key(seed)
        ks = jax.random.split(key, 5)
        s = 1.0 / np.sqrt(DM)
        x = jax.random.normal(ks[0], (B, N, DM), dtype=jnp.float32)
        Wq = jax.random.uniform(ks[1], (DM, DM), jnp.float32, -s, s)
        Wk = jax.random.uniform(ks[2], (DM, DM), jnp.float32, -s, s)
        Wv = jax.random.uniform(ks[3], (DM, DM), jnp.float32, -s, s)
        Wo = jax.random.uniform(ks[4], (DM, DM), jnp.float32, -s, s)
        return {'x': x, 'Wq': Wq, 'Wk': Wk, 'Wv': Wv, 'Wo': Wo}
    _L0_attn_in = _L0_attn_setup()

    def _L0_ffn_setup():
        import jax, jax.numpy as jnp
        import numpy as np
        INT4_QMAX = 7.0

        def simulate_quantize_int4(w):
            scale = jnp.max(jnp.abs(w)) / INT4_QMAX
            q = jnp.clip(jnp.round(w / scale), -8.0, 7.0)
            return q * scale
        key = jax.random.key(seed)
        k_x, k_w, k_bias, k_a, k_b = jax.random.split(key, 5)
        d_in, features, rank = (512, 512, 16)
        x = jax.random.normal(k_x, (4, 4096, d_in), dtype=jnp.float32)
        kernel = jax.random.normal(k_w, (d_in, features), dtype=jnp.float32)
        bias = jax.random.normal(k_bias, (features,), dtype=jnp.float32)
        a = jax.random.normal(k_a, (d_in, rank), dtype=jnp.float32) * (1.0 / np.sqrt(d_in))
        b = jax.random.normal(k_b, (rank, features), dtype=jnp.float32) * 0.01
        return {'x': x, 'kernel': kernel, 'bias': bias, 'a': a, 'b': b}
    _L0_ffn_in = _L0_ffn_setup()
    _d = {'L0_attn_x': _L0_attn_in['x'], 'L0_attn_Wq': _L0_attn_in['Wq'], 'L0_attn_Wk': _L0_attn_in['Wk'], 'L0_attn_Wv': _L0_attn_in['Wv'], 'L0_attn_Wo': _L0_attn_in['Wo'], 'L0_ffn_kernel': _L0_ffn_in['kernel'], 'L0_ffn_bias': _L0_ffn_in['bias'], 'L0_ffn_a': _L0_ffn_in['a'], 'L0_ffn_b': _L0_ffn_in['b']}
    _x0 = _d['L0_attn_x']
    _d['L0_attn_x'] = jax.random.normal(jax.random.fold_in(jax.random.key(seed), 1), (8, 1024, 512), dtype=_x0.dtype)
    del _x0
    return _d

def reference(L0_attn_x, L0_attn_Wq, L0_attn_Wk, L0_attn_Wv, L0_attn_Wo, L0_ffn_kernel, L0_ffn_bias, L0_ffn_a, L0_ffn_b):

    def _L0_attn_ref(x, Wq, Wk, Wv, Wo):
        import jax, jax.numpy as jnp
        import numpy as np
        B, N, DM, H = (1, 1024, 512, 16)
        CURV = 1.0
        b, n, d = x.shape
        hd = d // H

        def split_heads(t):
            return t.reshape(b, n, H, hd).transpose(0, 2, 1, 3)
        q = split_heads(x @ Wq.T)
        k = split_heads(x @ Wk.T)
        v = split_heads(x @ Wv.T)
        q_norm_sq = jnp.sum(q * q, axis=-1, keepdims=True)
        k_norm_sq = jnp.sum(k * k, axis=-1)[:, :, None, :]
        qk = jnp.einsum('bhnd,bhmd->bhnm', q, k)
        diff_sq = jnp.maximum(q_norm_sq + k_norm_sq - 2.0 * qk, 0.0)
        denom = jnp.maximum((1.0 - CURV * q_norm_sq) * (1.0 - CURV * k_norm_sq), 1e-06)
        cosh_arg = jnp.maximum(1.0 + 2.0 * CURV * diff_sq / denom, 1.0)
        distance = jnp.where(cosh_arg > 1.0, jnp.arccosh(jnp.maximum(cosh_arg, 1.0 + 1e-12)), 0.0)
        attn = jax.nn.softmax(-distance, axis=-1)
        out = jnp.einsum('bhnm,bhmd->bhnd', attn, v)
        out = out.transpose(0, 2, 1, 3).reshape(b, n, d)
        return out @ Wo.T

    def _L0_ffn_ref(x, kernel, bias, a, b):
        import jax, jax.numpy as jnp
        import numpy as np
        INT4_QMAX = 7.0

        def simulate_quantize_int4(w):
            scale = jnp.max(jnp.abs(w)) / INT4_QMAX
            q = jnp.clip(jnp.round(w / scale), -8.0, 7.0)
            return q * scale
        w = simulate_quantize_int4(kernel)
        y = jnp.einsum('bsd,df->bsf', x, w) + bias
        lora = jnp.einsum('bsr,rf->bsf', jnp.einsum('bsd,dr->bsr', x, a), b)
        return y + lora
    x = L0_attn_x
    xn = _layernorm(x, axis=-1)
    x = x + _L0_attn_ref(xn, L0_attn_Wq, L0_attn_Wk, L0_attn_Wv, L0_attn_Wo) + _L0_ffn_ref(xn, L0_ffn_kernel, L0_ffn_bias, L0_ffn_a, L0_ffn_b)
    return x

_drawn_inputs = setup_inputs


def setup_inputs(seed=0):
    import zlib

    import numpy as np

    out = dict(_drawn_inputs(seed))
    spreads = {}
    factors = {'L0_attn_Wq': 8.0,
     'L0_attn_Wk': 8.0,
     'L0_attn_Wv': 8.0,
     'L0_attn_Wo': 8.0,
     'L0_ffn_a': 8.0,
     'L0_ffn_b': 8.0}
    for name, (base, spread) in spreads.items():
        noise = np.random.default_rng([zlib.crc32(name.encode()), seed]).standard_normal(out[name].shape)
        drawn = base * np.exp(spread * noise) if base else spread * noise
        out[name] = jnp.asarray(drawn.astype(out[name].dtype))
    for name, factor in factors.items():
        out[name] = (out[name] * factor).astype(out[name].dtype)
    return out
```

```python
import concourse.bass as bass
from concourse import mybir
from contextlib import ExitStack

F32 = mybir.dt.float32
ALU = mybir.AluOpType
ACT = mybir.ActivationFunctionType
AX = mybir.AxisListType
ds = bass.ds

B, N, DM, H = 8, 1024, 512, 16
HD = DM // H
P = 128
T = B * N
KC = DM // P
NT = T // P
JC = N // P
HALF = 512
RANK = 16
EPS = 1e-5
ROUND = 1.5 * 2.0 ** 23


class Signals:

    def __init__(self, sem):
        self.sem, self.count = sem, 0

    def done(self, ins, by=1):
        ins.then_inc(self.sem, by)
        self.count += by
        return self.sem, self.count

    def start_over(self):
        self.count = 0


def wait(engine, *tickets):
    for sem, value in tickets:
        engine.wait_ge(sem, value)


def build(nc, x, wq_t, wk_t, wv_t, wo_t, ffn_w, bias, a_t, b, ident, out):
    ctx = ExitStack()
    with ctx:
        def sb(name, shape, dt=F32):
            return ctx.enter_context(nc.sbuf_tensor(name, shape, dt))

        def ps(name):
            return ctx.enter_context(nc.psum_tensor(name, [P, HALF], F32))

        sems = [ctx.enter_context(nc.semaphore(n)) for n in ("s_dma", "s_store", "s_pe", "s_act", "s_dve", "s_pool")]
        DMA, STORE, PE, AC, DV, PL = map(Signals, sems)

        def meet():
            nc.all_engine_barrier()
            for s in sems:
                nc.sync.sem_clear(s)
            nc.all_engine_barrier()
            for s in (DMA, STORE, PE, AC, DV, PL):
                s.start_over()

        q_t = nc.dram_tensor("q_t", [DM, T], F32).ap()
        k_t = nc.dram_tensor("k_t", [DM, T], F32).ap()
        v_d = nc.dram_tensor("v_d", [T, DM], F32).ap()
        res_d = nc.dram_tensor("res_d", [T, DM], F32).ap()
        att_d = nc.dram_tensor("att_d", [DM, T], F32).ap()

        Wq, Wk, Wv, Wo, Wf = (sb(n, [P, KC, DM]) for n in ("Wq", "Wk", "Wv", "Wo", "Wf"))
        At, Bl = sb("At", [RANK, DM]), sb("Bl", [RANK, DM])
        bias_b = sb("bias_b", [P, DM])
        idn = sb("idn", [P, P])
        ones = sb("ones", [P, P])
        eps = sb("eps", [P, 1])
        two = sb("two", [P, 1])
        t0, t1, t2, t3, t4, t5 = (sb(f"t{i}", [P, DM]) for i in range(6))
        xn_t = sb("xn_t", [P, KC, P])
        stats = sb("stats", [P, 6])
        mv = sb("mv", [P, 2])
        small = sb("small", [P, 8])
        pA, pB, pC, pD, pE = (ps(n) for n in ("pA", "pB", "pC", "pD", "pE"))

        def project(psum, lhs, rhs, free):
            for c in range(KC):
                last = nc.tensor.matmul(psum[:, :], lhs(c), rhs(c), start=c == 0, stop=c == KC - 1)
            return PE.done(last)

        loads = []
        for dst, src in ((Wq, wq_t), (Wk, wk_t), (Wv, wv_t), (Wo, wo_t), (Wf, ffn_w)):
            loads.append(DMA.done(nc.sync.dma_start(dst[:, :, :], src.rearrange("(c p) n -> p c n", p=P)), 16))
        for dst, src in ((At, a_t), (Bl, b), (bias_b, bias), (idn, ident)):
            loads.append(DMA.done(nc.sync.dma_start(dst[:, :], src), 16))
        loaded = loads[-1]
        DV.done(nc.vector.memset(ones[:, :], 1.0))
        DV.done(nc.vector.memset(eps[:, :], EPS))
        DV.done(nc.vector.memset(two[:, :], 2.0))
        wait(nc.vector, loaded)
        r = DV.done(nc.vector.tensor_reduce(small[:, 0:1], Wf[:, :, :], AX.XY, ALU.max, apply_absolute_value=True))
        wait(nc.gpsimd, r)
        r = PL.done(nc.gpsimd.partition_all_reduce(small[:, 1:2], small[:, 0:1], P, bass.bass_isa.ReduceOp.max))
        wait(nc.vector, r)
        r = DV.done(nc.vector.tensor_scalar(small[:, 2:3], small[:, 1:2], 1.0 / 7.0, None, ALU.mult))
        wait(nc.vector, r)
        r = DV.done(nc.vector.reciprocal(small[:, 3:4], small[:, 2:3]))
        wait(nc.vector, r)
        wait(nc.tensor, loaded)
        for c in range(KC):
            wait(nc.vector, r)
            r = DV.done(nc.vector.tensor_scalar(t0[:, :], Wf[:, c, :], small[:, 3:4], ROUND, ALU.mult, ALU.add))
            wait(nc.vector, r)
            r = DV.done(nc.vector.tensor_scalar(t1[:, :], t0[:, :], ROUND, -8.0, ALU.subtract, ALU.max))
            wait(nc.vector, r)
            r = DV.done(nc.vector.tensor_scalar(t0[:, :], t1[:, :], 7.0, small[:, 2:3], ALU.min, ALU.mult))
            if c:
                wait(nc.tensor, rr)
            m = PE.done(nc.tensor.matmul(pA[:, :], At[:, c * P:(c + 1) * P], Bl[:, :], start=True, stop=True))
            wait(nc.vector, r, m)
            r = rr = DV.done(nc.vector.tensor_tensor(Wf[:, c, :], pA[:, :], t0[:, :], ALU.add))
        meet()

        with nc.Fori(0, NT) as n:
            row = n * P
            ld = DMA.done(nc.sync.dma_start(t0[:, :], x[ds(row, P), :]), 16)
            wait(nc.vector, ld)
            wait(nc.vector, DV.done(nc.vector.bn_stats(stats[:, :], t0[:, :])))
            s = DV.done(nc.vector.bn_aggr(mv[:, :], stats[:, :]))
            wait(nc.scalar, s)
            s = AC.done(nc.scalar.activation(small[:, 0:1], mv[:, 1:2], ACT.Sqrt, bias=eps[:, 0:1]))
            wait(nc.vector, s)
            wait(nc.vector, DV.done(nc.vector.reciprocal(small[:, 1:2], small[:, 0:1])))
            wait(nc.vector, DV.done(nc.vector.tensor_scalar(small[:, 2:3], mv[:, 1:2], EPS, small[:, 1:2], ALU.add, ALU.mult)))
            wait(nc.vector, DV.done(nc.vector.tensor_scalar(small[:, 3:4], small[:, 2:3], small[:, 1:2], -0.5, ALU.mult, ALU.mult)))
            wait(nc.vector, DV.done(nc.vector.tensor_scalar(small[:, 4:5], small[:, 3:4], 1.5, small[:, 1:2], ALU.add, ALU.mult)))
            xn = DV.done(nc.vector.tensor_scalar(t1[:, :], t0[:, :], mv[:, 0:1], small[:, 4:5], ALU.subtract, ALU.mult))
            xb = DV.done(nc.vector.tensor_tensor(t2[:, :], t0[:, :], bias_b[:, :], ALU.add))
            wait(nc.tensor, xn)
            for c in range(KC):
                m = nc.tensor.transpose(pA[:, c * P:(c + 1) * P], t1[:, c * P:(c + 1) * P], idn[:, :])
            m = PE.done(m)
            wait(nc.vector, m)
            xt = DV.done(nc.vector.tensor_copy(xn_t[:, :, :], pA[:, :].rearrange("p (c n) -> p c n", c=KC)))
            wait(nc.tensor, xt)
            for psum, W, hold, dst in ((pB, Wq, t3, q_t), (pC, Wk, t4, k_t)):
                for o in range(KC):
                    for c in range(KC):
                        m = nc.tensor.matmul(psum[:, o * P:(o + 1) * P], W[:, c, o * P:(o + 1) * P], xn_t[:, c, :],
                                             start=c == 0, stop=c == KC - 1)
                wait(nc.vector, PE.done(m))
                cp = DV.done(nc.vector.tensor_copy(hold[:, :], psum[:, :]))
                wait(nc.sync, cp)
                st = STORE.done(nc.sync.dma_start(dst.rearrange("(c p) n -> p c n", p=P)[:, :, ds(row, P)],
                                                  hold[:, :].rearrange("p (c n) -> p c n", c=KC)), 16)
            m = project(pD, lambda c: xn_t[:, c, :], lambda c: Wv[:, c, :], DM)
            wait(nc.vector, m)
            cp = DV.done(nc.vector.tensor_copy(t5[:, :], pD[:, :]))
            wait(nc.sync, cp)
            STORE.done(nc.sync.dma_start(v_d[ds(row, P), :], t5[:, :]), 16)
            m = project(pE, lambda c: xn_t[:, c, :], lambda c: Wf[:, c, :], DM)
            wait(nc.vector, m, xb)
            cp = DV.done(nc.vector.tensor_tensor(t1[:, :], pE[:, :], t2[:, :], ALU.add))
            wait(nc.sync, cp)
            st = STORE.done(nc.sync.dma_start(res_d[ds(row, P), :], t1[:, :]), 16)
            wait(nc.sync, st)
            meet()

        KF, QF = sb("KF", [96, N]), sb("QF", [96, N])
        Kh, Qh, sq = sb("Kh", [HD, N]), sb("Qh", [HD, N]), sb("sq", [HD, 2, N])
        Vh = sb("Vh", [P, JC, HD])
        a_b, b_p = sb("a_b", [P, N]), sb("b_p", [P, JC])
        o_sb = sb("o_sb", [HD, N])
        DV.done(nc.vector.memset(KF[:, :], 0.0))
        DV.done(nc.vector.memset(QF[:, :], 0.0))
        wait(nc.vector, (DV.sem, DV.count))
        DV.done(nc.vector.memset(KF[32:33, :], 1.0))
        DV.done(nc.vector.memset(QF[64:65, :], 1.0))
        meet()
        with nc.Fori(0, B) as bi:
            with nc.Fori(0, H) as h:
                col, feat = bi * N, h * HD
                DMA.done(nc.sync.dma_start(Kh[:, :], k_t[ds(feat, HD), ds(col, N)]), 16)
                DMA.done(nc.sync.dma_start(QF[0:HD, :], q_t[ds(feat, HD), ds(col, N)]), 16)
                ld = DMA.done(nc.sync.dma_start(Vh[:, :, :], v_d[ds(col, N), ds(feat, HD)].rearrange("(j p) d -> p j d", p=P)), 16)
                wait(nc.vector, ld)
                DV.done(nc.vector.tensor_scalar(KF[0:HD, :], Kh[:, :], -2.0, None, ALU.mult))
                DV.done(nc.vector.tensor_tensor(sq[:, 0, :], Kh[:, :], Kh[:, :], ALU.mult))
                s = DV.done(nc.vector.tensor_tensor(sq[:, 1, :], QF[0:HD, :], QF[0:HD, :], ALU.mult))
                wait(nc.tensor, s)
                for i in range(2):
                    cols = slice(i * HALF, (i + 1) * HALF)
                    nc.tensor.matmul(pA[32:64, :], ones[0:HD, 0:32], sq[:, 1, cols], start=True, stop=True)
                    nc.tensor.matmul(pA[64:96, :], ones[0:HD, 0:32], sq[:, 0, cols], start=True, stop=True)
                    m = PE.done(nc.tensor.matmul(pB[:, :], ones[0:HD, :], sq[:, 1, cols], start=True, stop=True))
                    wait(nc.vector, m)
                    DV.done(nc.vector.tensor_copy(QF[32:33, cols], pA[32:33, :]))
                    DV.done(nc.vector.tensor_copy(KF[64:65, cols], pA[64:65, :]))
                    s = DV.done(nc.vector.tensor_scalar(a_b[:, cols], pB[:, :], -1.0, 1.0, ALU.mult, ALU.add))
                    wait(nc.tensor, s)
                for j in range(JC):
                    m = nc.tensor.matmul(pC[:, j:j + 1], sq[:, 0, j * P:(j + 1) * P], ones[0:HD, 0:1], start=True, stop=True)
                wait(nc.vector, PE.done(m))
                s = DV.done(nc.vector.tensor_scalar(b_p[:, :], pC[:, 0:JC], -1.0, 1.0, ALU.mult, ALU.add))
                wait(nc.vector, s)
                for i in range(2):
                    cols = slice(i * HALF, (i + 1) * HALF)
                    for j in range(JC):
                        m = PE.done(nc.tensor.matmul(pA[:, :], KF[:, j * P:(j + 1) * P], QF[:, cols], start=True, stop=True))
                        wait(nc.vector, DV.done(nc.vector.tensor_scalar(t0[:, :], a_b[:, cols], b_p[:, j:j + 1], 1e-6, ALU.mult, ALU.max)))
                        wait(nc.vector, DV.done(nc.vector.reciprocal(t1[:, :], t0[:, :])))
                        wait(nc.vector, m)
                        u = DV.done(nc.vector.scalar_tensor_tensor(out=t2[:, :], in0=pA[:, :], scalar=0.0, in1=t1[:, :], op0=ALU.max, op1=ALU.mult))
                        wait(nc.scalar, u)
                        AC.done(nc.scalar.activation(t3[:, :], t2[:, :], ACT.Sqrt, scale=2.0))
                        s = AC.done(nc.scalar.activation(t4[:, :], t2[:, :], ACT.Sqrt, scale=2.0, bias=two[:, 0:1]))
                        wait(nc.vector, s)
                        wait(nc.vector, DV.done(nc.vector.tensor_tensor(t5[:, :], t3[:, :], t4[:, :], ALU.mult)))
                        wait(nc.vector, DV.done(nc.vector.scalar_tensor_tensor(out=t0[:, :], in0=t2[:, :], scalar=2.0, in1=t5[:, :], op0=ALU.mult, op1=ALU.add)))
                        wait(nc.vector, DV.done(nc.vector.tensor_scalar(t1[:, :], t0[:, :], 1.0, None, ALU.add)))
                        w = DV.done(nc.vector.reciprocal(t0[:, :], t1[:, :]))
                        wait(nc.tensor, w)
                        nc.tensor.matmul(pD[0:HD, :], Vh[:, j, :], t0[:, :], start=j == 0, stop=j == JC - 1)
                        m = PE.done(nc.tensor.matmul(pE[0:HD, :], ones[:, 0:HD], t0[:, :], start=j == 0, stop=j == JC - 1))
                        wait(nc.vector, m)
                    s = DV.done(nc.vector.reciprocal(t1[0:HD, :], pE[0:HD, :]))
                    wait(nc.vector, s)
                    s = DV.done(nc.vector.tensor_tensor(o_sb[:, cols], pD[0:HD, :], t1[0:HD, :], ALU.mult))
                    wait(nc.tensor, s)
                    wait(nc.vector, s)
                wait(nc.sync, s)
                wait(nc.sync, STORE.done(nc.sync.dma_start(att_d[ds(feat, HD), ds(col, N)], o_sb[:, :]), 16))
                meet()

        with nc.Fori(0, NT) as n:
            row = n * P
            DMA.done(nc.sync.dma_start(xn_t[:, :, :], att_d.rearrange("(c p) n -> p c n", p=P)[:, :, ds(row, P)]), 16)
            ld = DMA.done(nc.sync.dma_start(t0[:, :], res_d[ds(row, P), :]), 16)
            wait(nc.tensor, ld)
            m = project(pA, lambda c: xn_t[:, c, :], lambda c: Wo[:, c, :], DM)
            wait(nc.vector, m, ld)
            s = DV.done(nc.vector.tensor_tensor(t1[:, :], pA[:, :], t0[:, :], ALU.add))
            wait(nc.sync, s)
            wait(nc.sync, STORE.done(nc.sync.dma_start(out[ds(row, P), :], t1[:, :]), 16))
            meet()


def kernel(L0_attn_x, L0_attn_Wq, L0_attn_Wk, L0_attn_Wv, L0_attn_Wo, L0_ffn_kernel, L0_ffn_bias, L0_ffn_a, L0_ffn_b):
    import numpy as np
    import concourse.bacc as bacc
    from concourse.bass_utils import run_bass_kernel_spmd

    lay = np.ascontiguousarray
    arrays = {
        "x": lay(np.asarray(L0_attn_x).reshape(T, DM)),
        "wq_t": lay(np.asarray(L0_attn_Wq).T), "wk_t": lay(np.asarray(L0_attn_Wk).T),
        "wv_t": lay(np.asarray(L0_attn_Wv).T), "wo_t": lay(np.asarray(L0_attn_Wo).T),
        "ffn_w": lay(L0_ffn_kernel),
        "bias": lay(np.broadcast_to(np.asarray(L0_ffn_bias), (P, DM))),
        "a_t": lay(np.asarray(L0_ffn_a).T), "b": lay(L0_ffn_b),
        "ident": np.eye(P, dtype=np.float32),
    }
    nc = bacc.Bacc("TRN2", target_bir_lowering=False, num_devices=1)
    args = {k: nc.dram_tensor(f"in_{k}", a.shape, F32, kind="ExternalInput").ap() for k, a in arrays.items()}
    out = nc.dram_tensor("out_0", (T, DM), F32, kind="ExternalOutput").ap()
    build(nc, out=out, **args)
    r = run_bass_kernel_spmd(nc, [{f"in_{k}": a for k, a in arrays.items()}], core_ids=[0])
    return r.results[0]["out_0"].reshape(B, N, DM)
```

```python
import concourse.bass as bass
from concourse import mybir
from contextlib import ExitStack

F32, F16, I32 = mybir.dt.float32, mybir.dt.float16, mybir.dt.int32
ALU = mybir.AluOpType
ACT = mybir.ActivationFunctionType
AX = mybir.AxisListType
ds = bass.ds

B, N, DM, H = 8, 1024, 512, 16
HD = DM // H
P = 128
T = B * N
KC = DM // P
G4 = P // HD
NT = T // P
JC = N // P
HALF = 512
BLK = 512
TPB = BLK // P
NB = T // BLK
RANK = 16
EPS = 1e-5
ROUND = 1.5 * 2.0 ** 23
AUG = 8
ROWS = 3 * HD + AUG
RS = 64.0
CS = RS * RS / 2
NORM_MIN = 16.0
W_TOP = 16.0
LEAD = 3
LATE = 2
POOL_COLS = 1408


class Signals:

    def __init__(self, sem):
        self.sem, self.count = sem, 0

    def done(self, ins, by=1):
        ins.then_inc(self.sem, by)
        self.count += by
        return self.sem, self.count


def wait(engine, *tickets):
    for t in tickets:
        if t is not None:
            engine.wait_ge(*t)


def build(nc, x, wq_t, wk_t, wv_t, wo_t, ffn_w, bias, a_t, b, ident, out):
    ctx = ExitStack()
    with ctx:
        names = ("pe", "act", "dve", "pool", "load", "x", "stack0", "stack1", "feat", "v", "res",
                 "att", "z", "rz", "norm", "raw", "resin0", "resin1", "out0", "out1")
        sems = [ctx.enter_context(nc.semaphore("s_" + n)) for n in names]
        S = {n: Signals(s) for n, s in zip(names, sems)}
        PE, AC, DV, PL = (S[n] for n in ("pe", "act", "dve", "pool"))
        dma = {n: S[n] for n in names[4:]}

        def meet():
            for s in dma.values():
                if s.count:
                    nc.sync.wait_ge(s.sem, s.count)
            nc.all_engine_barrier()
            for s in S.values():
                if s.count:
                    nc.sync.sem_clear(s.sem)
                s.count = 0
            nc.all_engine_barrier()

        def load(name, dst, src):
            return S[name].done(nc.sync.dma_start(dst, src), 16)

        def on_dve(ins):
            t = DV.done(ins)
            wait(nc.vector, t)
            return t

        def scratch(name, shape, dt):
            return nc.dram_tensor(name, shape, dt).ap()

        feat_d = {k: scratch(f"{k}_d", [NB * DM, BLK], F16) for k in ("qh", "ql", "kh", "kl")}
        aug_d = {k: scratch(f"aug_{k}_d", [NB * P, BLK], F16) for k in "qk"}
        v_d = scratch("v_d", [T, DM], F32)
        res_d = scratch("res_d", [T, DM], F32)
        att_d = scratch("att_d", [NB * DM, BLK], F32)
        z_d = scratch("z_d", [NB * H, BLK], F32)
        rz_d = scratch("rz_d", [NB * H, BLK], F32)

        outer_sb = lambda name, shape, dt=F32: ctx.enter_context(nc.sbuf_tensor(name, shape, dt))
        scale = outer_sb("scale", [P, 16])
        flag = outer_sb("flag", [P, 2 * H])
        flag_all = outer_sb("flag_all", [P, 2])
        flag_int = outer_sb("flag_int", [P, 1], I32)
        IQ, IK, IV, IO, IF, IVO = 5, 6, 7, 8, 9, 10

        env = dict(locals())
        fast(nc, env)

        r = DV.done(nc.vector.tensor_reduce(flag_all[:, 0:1], flag[:, :], AX.X, ALU.max))
        wait(nc.gpsimd, r)
        r = PL.done(nc.gpsimd.partition_all_reduce(flag_all[:, 1:2], flag_all[:, 0:1], P, bass.bass_isa.ReduceOp.max))
        wait(nc.vector, r)
        DV.done(nc.vector.tensor_copy(flag_int[:, :], flag_all[:, 1:2]))
        wait(nc.vector, (DV.sem, DV.count))
        meet()
        small_norm = nc.values_load(flag_int[0:1, 0:1], min_val=0, max_val=1)
        with nc.If(small_norm > 0):
            general(nc, env)
        nc.end_ifs()


def fast(nc, e):
    S, PE, AC, DV, PL = e["S"], e["PE"], e["AC"], e["DV"], e["PL"]
    meet, load, on_dve = e["meet"], e["load"], e["on_dve"]
    feat_d, aug_d, v_d, res_d, att_d, z_d, rz_d = (e[k] for k in ("feat_d", "aug_d", "v_d", "res_d", "att_d", "z_d", "rz_d"))
    x, out, scale, flag = e["x"], e["out"], e["scale"], e["flag"]
    IQ, IK, IV, IO, IF, IVO = (e[k] for k in ("IQ", "IK", "IV", "IO", "IF", "IVO"))
    with ExitStack() as ctx:
        def sb(name, shape, dt=F32):
            return ctx.enter_context(nc.sbuf_tensor(name, shape, dt))

        def ps(name, cols=HALF):
            return ctx.enter_context(nc.psum_tensor(name, [P, cols], F32))

        W = {k: (sb(f"W{k}h", [P, KC, DM], F16), sb(f"W{k}l", [P, KC, DM], F16)) for k in "qkvof"}
        bias_b, idn, idn16, ones = sb("bias_b", [P, DM]), sb("idn", [P, P]), sb("idn16", [P, P], F16), sb("ones", [P, HD])
        QS = [sb(f"QS{i}", [ROWS, G4, N], F16) for i in range(2)]
        KS = [sb(f"KS{i}", [ROWS, G4, N], F16) for i in range(2)]
        VS = [sb(f"VS{i}", [P, JC, P]) for i in range(2)]
        cosh = sb("cosh", [P, 4, G4 * HALF])
        root = sb("root", [P, 3, G4 * HALF])
        xt = sb("xt", [P, TPB, DM])
        xn = sb("xn", [P, 2, DM])
        xh, xl = sb("xh", [P, 2, KC, P], F16), sb("xl", [P, 2, KC, P], F16)
        qk = sb("qk", [P, 2, DM])
        sqr = sb("sqr", [P, DM])
        aug = sb("aug", [P, 2, H, AUG], F16)
        feat = {k: sb(f"feat_{k}", [P, KC, 2 * P], F16) for k in ("qh", "ql", "kh", "kl")}
        aug_o = sb("aug_o", [P, 2, 2 * P], F16)
        v_o, f_o = sb("v_o", [P, DM]), sb("f_o", [P, DM])
        stats, mv, ln = sb("stats", [P, TPB, 6]), sb("mv", [P, TPB, 2]), sb("ln", [P, 5, TPB])
        nrm, rcp = sb("nrm", [P, 2, H]), sb("rcp", [P, 3, 2, H])
        o_s, z_s = sb("o_s", [P, HALF]), sb("z_s", [P, HALF])
        raw, rzb = sb("raw", [P, KC, 2 * P]), sb("rzb", [P, KC, 2 * P])
        zc = sb("zc", [P, 2, BLK * H // P])
        ah, al = sb("ah", [P, KC, BLK], F16), sb("al", [P, KC, BLK], F16)
        res_i, out_o = sb("res_i", [P, 2, DM]), sb("out_o", [P, 2, DM])
        pU = ps("pU", 4 * HALF)
        pO, pZ = ps("pO"), ps("pZ")
        pM = [ps("pM0"), ps("pM1")]

        W32 = {k: cosh[:, i, :].rearrange("p (c n) -> p c n", c=KC) for i, k in enumerate("qkvo")}
        W32["f"] = root[:, 0, :].rearrange("p (c n) -> p c n", c=KC)
        tmp = root[:, 1, :].rearrange("p (c n) -> p c n", c=KC)
        At, Bl = root[0:RANK, 2, 0:DM], root[0:RANK, 2, DM:2 * DM]
        for k, src in zip("qkvof", (e["wq_t"], e["wk_t"], e["wv_t"], e["wo_t"], e["ffn_w"])):
            load("load", W32[k], src.rearrange("(c p) n -> p c n", p=P))
        load("load", At, e["a_t"])
        load("load", Bl, e["b"])
        load("load", bias_b[:, :], e["bias"])
        loaded = load("load", idn[:, :], e["ident"])
        DV.done(nc.vector.memset(ones[:, :], 1.0))
        DV.done(nc.vector.memset(flag[:, :], 0.0))
        a = on_dve(nc.vector.memset(aug[:, :, :, :], 0.0))
        DV.done(nc.vector.memset(aug[:, 0, :, 6:7], RS))
        DV.done(nc.vector.memset(aug[:, 1, :, 6:7], CS / RS))
        wait(nc.vector, loaded)
        DV.done(nc.vector.tensor_copy(idn16[:, :], idn[:, :]))
        top = sb("top", [P, 12])
        topi = top[:, :].bitcast(I32)
        r = DV.done(nc.vector.tensor_reduce(top[:, 0:1], W32["f"], AX.XY, ALU.max, apply_absolute_value=True))
        wait(nc.gpsimd, r)
        r = PL.done(nc.gpsimd.partition_all_reduce(top[:, 1:2], top[:, 0:1], P, bass.bass_isa.ReduceOp.max))
        wait(nc.vector, r)
        on_dve(nc.vector.tensor_scalar(top[:, 2:3], top[:, 1:2], 1.0 / 7.0, None, ALU.mult))
        on_dve(nc.vector.reciprocal(top[:, 3:4], top[:, 2:3]))
        wait(nc.tensor, loaded)
        for c in range(KC):
            on_dve(nc.vector.tensor_scalar(tmp[:, c, :], W32["f"][:, c, :], top[:, 3:4], ROUND, ALU.mult, ALU.add))
            on_dve(nc.vector.tensor_scalar(tmp[:, c, :], tmp[:, c, :], ROUND, -8.0, ALU.subtract, ALU.max))
            on_dve(nc.vector.tensor_scalar(tmp[:, c, :], tmp[:, c, :], 7.0, top[:, 2:3], ALU.min, ALU.mult))
            if c > 1:
                wait(nc.tensor, added[c - 2])
            else:
                added = []
            m = PE.done(nc.tensor.matmul(pM[c % 2][:, :], At[:, c * P:(c + 1) * P], Bl, start=True, stop=True))
            wait(nc.vector, m)
            added.append(on_dve(nc.vector.tensor_tensor(W32["f"][:, c, :], pM[c % 2][:, :], tmp[:, c, :], ALU.add)))
        for i, k in enumerate("qkvof"):
            r = DV.done(nc.vector.tensor_reduce(top[:, 4 + i:5 + i], W32[k], AX.XY, ALU.max, apply_absolute_value=True))
        wait(nc.gpsimd, r)
        r = PL.done(nc.gpsimd.partition_all_reduce(scale[:, 0:5], top[:, 4:9], P, bass.bass_isa.ReduceOp.max))
        wait(nc.vector, r)
        on_dve(nc.vector.tensor_scalar(top[:, 4:9], scale[:, 0:5], 2.0 ** -100, 2.0 ** 100, ALU.max, ALU.min))
        on_dve(nc.vector.tensor_scalar(topi[:, 4:9], topi[:, 4:9], 0x7F800000, None, ALU.bitwise_and))
        on_dve(nc.vector.tensor_scalar(scale[:, IQ:IQ + 5], top[:, 4:9], 1.0 / W_TOP, None, ALU.mult))
        on_dve(nc.vector.reciprocal(scale[:, 0:5], scale[:, IQ:IQ + 5]))
        on_dve(nc.vector.tensor_tensor(scale[:, IVO:IVO + 1], scale[:, IV:IV + 1], scale[:, IO:IO + 1], ALU.mult))
        for i, k in enumerate("qkvof"):
            on_dve(nc.vector.tensor_scalar(W32[k], W32[k], scale[:, i:i + 1], None, ALU.mult))
            on_dve(nc.vector.tensor_copy(W[k][0][:, :, :], W32[k]))
            on_dve(nc.vector.tensor_tensor(W[k][1][:, :, :], W32[k], W[k][0][:, :, :], ALU.subtract))
        meet()


        class Misc:

            def __init__(self):
                self.n, self.readers = 0, [[], []]

            def take(self):
                i = self.n % 2
                self.n += 1
                wait(nc.tensor, *self.readers[i])
                self.readers[i] = []
                return i

        def product(bank, hi, lo, w, start=0):
            for c in range(KC):
                wh, wl = w[0][:, c, :], w[1][:, c, :]
                nc.tensor.matmul(bank[:, :], hi(c), wh, start=c == 0, stop=False)
                nc.tensor.matmul(bank[:, :], hi(c), wl, start=False, stop=False)
                last = nc.tensor.matmul(bank[:, :], lo(c), wh, start=False, stop=c == KC - 1)
            return PE.done(last)

        def projections(blk, misc, L):
            units = []
            t = {}
            t["x"] = load("x", xt[:, :, :], x[ds(blk * BLK, BLK), :].rearrange("(i p) n -> p i n", p=P))

            def norms():
                wait(nc.vector, t["x"])
                for i in range(TPB):
                    r = DV.done(nc.vector.bn_stats(stats[:, i, :], xt[:, i, :]))
                wait(nc.vector, r)
                for i in range(TPB):
                    r = DV.done(nc.vector.bn_aggr(mv[:, i, :], stats[:, i, :]))
                wait(nc.vector, r)
                r = on_dve(nc.vector.tensor_scalar(ln[:, 0, :], mv[:, :, 1], EPS, None, ALU.add))
                wait(nc.scalar, r)
                r = AC.done(nc.scalar.activation(ln[:, 1, :], ln[:, 0, :], ACT.Sqrt))
                wait(nc.vector, r)
                on_dve(nc.vector.reciprocal(ln[:, 2, :], ln[:, 1, :]))
                on_dve(nc.vector.tensor_tensor(ln[:, 3, :], ln[:, 2, :], ln[:, 2, :], ALU.mult))
                on_dve(nc.vector.tensor_tensor(ln[:, 4, :], ln[:, 3, :], ln[:, 0, :], ALU.mult))
                on_dve(nc.vector.tensor_scalar(ln[:, 3, :], ln[:, 4, :], -0.5, 1.5, ALU.mult, ALU.add))
                on_dve(nc.vector.tensor_tensor(ln[:, 1, :], ln[:, 2, :], ln[:, 3, :], ALU.mult))
                normalise(0)

            def normalise(i):
                wait(nc.vector, t.get(("T", i - 2)))
                t["xn", i] = DV.done(nc.vector.tensor_scalar(xn[:, i % 2, :], xt[:, i, :], mv[:, i, 0:1], ln[:, 1, i:i + 1],
                                                             ALU.subtract, ALU.mult))
                wait(nc.gpsimd, t["xn", i])
                t["xb", i] = PL.done(nc.gpsimd.tensor_tensor(xt[:, i, :], xt[:, i, :], bias_b[:, :], ALU.add))

            def transposes(i):
                def fill():
                    k = t["bank"] = misc.take()
                    wait(nc.tensor, t["xn", i])
                    for c in range(KC):
                        m = nc.tensor.transpose(pM[k][:, c * P:(c + 1) * P], xn[:, i % 2, c * P:(c + 1) * P], idn[:, :])
                    t["T", i] = PE.done(m)

                def empty(k):
                    v = pM[k][:, :].rearrange("p (c n) -> p c n", c=KC)
                    wait(nc.scalar, t["T", i], t.get(("F", i - 2)))
                    r = AC.done(nc.scalar.copy(xh[:, i % 2, :, :], v))
                    wait(nc.vector, r)
                    t["xT", i] = DV.done(nc.vector.tensor_tensor(xl[:, i % 2, :, :], v, xh[:, i % 2, :, :], ALU.subtract))
                    misc.readers[k] = [r, t["xT", i]]
                    if i + 1 < TPB:
                        normalise(i + 1)
                return fill, empty

            def unit(i, key):
                def fill():
                    k = t["bank"] = misc.take()
                    wait(nc.tensor, t["xT", i])
                    t[key.upper(), i] = product(pM[k], lambda c: xh[:, i % 2, c, :], lambda c: xl[:, i % 2, c, :], W[key])
                return fill

            def qk_unit(i, s):
                key = "qk"[s]

                def empty(k):
                    wait(nc.scalar, t[key.upper(), i], t.get(("TX", s, i - 1)), t.get(("sum", 1 - s, i - 1 + s)))
                    r = AC.done(nc.scalar.activation(qk[:, s, :], pM[k][:, :], ACT.Copy, scale=scale[:, IQ + s:IQ + s + 1]))
                    misc.readers[k] = [r]
                    wait(nc.scalar, r)
                    r = AC.done(nc.scalar.activation(sqr[:, :], qk[:, s, :], ACT.Square))
                    wait(nc.vector, r, t.get(("augd", i - 1)))
                    t["sum", s, i] = DV.done(nc.vector.tensor_reduce(nrm[:, s, :], sqr[:, :].rearrange("p (h d) -> p h d", h=H), AX.X, ALU.add))
                    if s == 1:
                        features(i)
                return unit(i, key), empty

            def features(i):
                wait(nc.vector, t["sum", 1, i])
                fl = flag[:, :].rearrange("p (s h) -> p s h", s=2)
                DV.done(nc.vector.scalar_tensor_tensor(out=fl, in0=nrm[:, :, :], scalar=NORM_MIN, in1=fl, op0=ALU.is_lt, op1=ALU.max))
                on_dve(nc.vector.tensor_scalar(rcp[:, 0, :, :], nrm[:, :, :], -1.0 / RS, 1.0 / RS, ALU.mult, ALU.add))
                on_dve(nc.vector.reciprocal(rcp[:, 1, :, :], rcp[:, 0, :, :]))
                r = on_dve(nc.vector.tensor_tensor(rcp[:, 2, :, :], nrm[:, :, :], rcp[:, 1, :, :], ALU.mult))
                R, M = rcp[:, 1, :, :], rcp[:, 2, :, :]
                v = qk[:, :, :].rearrange("p s (h d) -> p s h d", h=H)
                bc = lambda s: R[:, s, :].unsqueeze(2).to_broadcast([P, H, HD])
                DV.done(nc.vector.scalar_tensor_tensor(out=v[:, 0], in0=v[:, 0], scalar=-2.0, in1=bc(0), op0=ALU.mult, op1=ALU.mult))
                t["scaled", i] = DV.done(nc.vector.tensor_tensor(v[:, 1], v[:, 1], bc(1), ALU.mult))
                wait(nc.vector, t.get(("AU", i - 1)))
                two = lambda a: a.unsqueeze(2).to_broadcast([P, H, 2])
                one = lambda a: a.unsqueeze(2)
                q, k = aug[:, 0, :, :], aug[:, 1, :, :]
                DV.done(nc.vector.tensor_copy(q[:, :, 0:2], two(M[:, 0, :])))
                DV.done(nc.vector.tensor_copy(q[:, :, 3:5], two(R[:, 0, :])))
                DV.done(nc.vector.tensor_copy(k[:, :, 0:3:2], two(R[:, 1, :])))
                r = DV.done(nc.vector.tensor_copy(k[:, :, 3:6:2], two(M[:, 1, :])))
                wait(nc.vector, r)
                for dst, full, high in ((q[:, :, 2:3], M[:, 0, :], q[:, :, 0:1]), (q[:, :, 5:6], R[:, 0, :], q[:, :, 3:4]),
                                        (k[:, :, 1:2], R[:, 1, :], k[:, :, 0:1]), (k[:, :, 4:5], M[:, 1, :], k[:, :, 3:4])):
                    r = DV.done(nc.vector.tensor_tensor(dst, one(full), high, ALU.subtract))
                t["augd", i] = r

            def v_unit(i):
                def empty(k):
                    wait(nc.scalar, t["V", i], t.get("v_stored"))
                    r = AC.done(nc.scalar.copy(v_o[:, :], pM[k][:, :]))
                    misc.readers[k] = [r]
                    wait(nc.sync, r)
                    t["v_stored"] = load("v", v_d[ds(blk * BLK + i * P, P), :], v_o[:, :])
                return unit(i, "v"), empty

            def f_unit(i):
                def empty(k):
                    wait(nc.vector, t["F", i], t["xb", i], t.get("f_stored"))
                    r = DV.done(nc.vector.scalar_tensor_tensor(out=f_o[:, :], in0=pM[k][:, :], scalar=scale[:, IF:IF + 1],
                                                               in1=xt[:, i, :], op0=ALU.mult, op1=ALU.add))
                    misc.readers[k] = [r]
                    wait(nc.sync, r)
                    t["f_stored"] = load("res", res_d[ds(blk * BLK + i * P, P), :], f_o[:, :])
                return unit(i, "f"), empty

            def feature_unit(i, s):
                key = "qk"[s]

                def fill():
                    k = t["bank"] = misc.take()
                    wait(nc.tensor, t["scaled", i])
                    for c in range(KC):
                        m = nc.tensor.transpose(pM[k][:, c * P:(c + 1) * P], qk[:, s, c * P:(c + 1) * P], idn[:, :])
                    t["TX", s, i] = PE.done(m)

                def empty(k):
                    v = pM[k][:, :].rearrange("p (c n) -> p c n", c=KC)
                    cols = slice((i % 2) * P, (i % 2 + 1) * P)
                    fh, fl = feat[key + "h"][:, :, cols], feat[key + "l"][:, :, cols]
                    if i % 2 == 0:
                        wait(nc.scalar, t.get("feat_stored"))
                    wait(nc.scalar, t["TX", s, i])
                    r = AC.done(nc.scalar.copy(fh, v))
                    wait(nc.vector, r)
                    t["fl", s, i] = DV.done(nc.vector.tensor_tensor(fl, v, fh, ALU.subtract))
                    misc.readers[k] = [r, t["fl", s, i]]
                return fill, empty

            def aug_unit(i):
                def fill():
                    k = t["bank"] = misc.take()
                    wait(nc.tensor, t["augd", i])
                    half = pM[k][:, 0:P].bitcast(F16)
                    for s in range(2):
                        m = nc.tensor.transpose(half[:, s * P:(s + 1) * P], aug[:, s, :, :].rearrange("p h r -> p (h r)"), idn16[:, :])
                    t["AU", i] = PE.done(m)

                def empty(k):
                    half = pM[k][:, 0:P].bitcast(F16).rearrange("p (s n) -> p s n", s=2)
                    wait(nc.scalar, t["AU", i])
                    r = AC.done(nc.scalar.copy(aug_o[:, :, (i % 2) * P:(i % 2 + 1) * P], half))
                    misc.readers[k] = [r]
                    if i % 2:
                        cols = slice((i // 2) * 2 * P, (i // 2 + 1) * 2 * P)
                        wait(nc.sync, r, t["fl", 0, i], t["fl", 1, i])
                        for key, f in feat.items():
                            load("feat", feat_d[key][ds(blk * DM, DM), cols].rearrange("(g p) n -> p g n", p=P), f[:, :, :])
                        for s in range(2):
                            t["feat_stored"] = load("feat", aug_d["qk"[s]][ds(blk * P, P), cols], aug_o[:, s, :])
                return fill, empty

            units.append((None, lambda k: norms()))
            units.append(transposes(0))
            units.append((None, None))
            for i in range(TPB):
                units += [qk_unit(i, 0), qk_unit(i, 1), v_unit(i), f_unit(i)]
                units.append(transposes(i + 1) if i + 1 < TPB else (None, None))
                units += [feature_unit(i, 0), feature_unit(i, 1), aug_unit(i)]
            L["units"] += [(f, g, t) for f, g in units]

        def output(blk, misc, L):
            t = {}
            rows = ds(blk * H, H)
            flat = lambda d: d[rows, :].rearrange("r (q n) -> (r q) n", q=P // H)

            def divisors():
                t["z"] = load("z", zc[:, 0, :], flat(z_d))
                wait(nc.vector, t["z"])
                r = DV.done(nc.vector.reciprocal(zc[:, 1, :], zc[:, 0, :]))
                wait(nc.sync, r)
                t["rz"] = load("rz", flat(rz_d), zc[:, 1, :])
                fetch(0)

            def fetch(i):
                cols = slice(i * 2 * P, (i + 1) * 2 * P)
                load("raw", raw[:, :, :], att_d[ds(blk * DM, DM), cols].rearrange("(g p) n -> p g n", p=P))
                wait(nc.sync, t["rz"])
                for h in range(G4):
                    src = rz_d[rows, cols].rearrange("(g h) n -> h g n", h=G4)[h:h + 1].to_broadcast([HD, KC, 2 * P])
                    t["raw", i] = load("raw", rzb[h * HD:(h + 1) * HD, :, :], src)

            def divide(i):
                cols = slice(i * 2 * P, (i + 1) * 2 * P)
                wait(nc.vector, t["raw", i])
                on_dve(nc.vector.tensor_tensor(raw[:, :, :], raw[:, :, :], rzb[:, :, :], ALU.mult))
                on_dve(nc.vector.tensor_copy(ah[:, :, cols], raw[:, :, :]))
                t["a", i] = DV.done(nc.vector.tensor_tensor(al[:, :, cols], raw[:, :, :], ah[:, :, cols], ALU.subtract))
                if i == 0:
                    wait(nc.sync, t["a", 0])
                    fetch(1)

            def tile(i):
                cols = slice(i * P, (i + 1) * P)

                def fill():
                    k = t["bank"] = misc.take()
                    wait(nc.tensor, t["a", i // 2])
                    wait(nc.sync, t.get(("sum", i - 2)))
                    t["res", i] = load(f"resin{i % 2}", res_i[:, i % 2, :], res_d[ds(blk * BLK + i * P, P), :])
                    t["O", i] = product(pM[k], lambda c: ah[:, c, cols], lambda c: al[:, c, cols], W["o"])

                def empty(k):
                    wait(nc.vector, t["O", i], t["res", i], t.get(("stored", i - 2)))
                    t["sum", i] = DV.done(nc.vector.scalar_tensor_tensor(out=out_o[:, i % 2, :], in0=pM[k][:, :], scalar=scale[:, IVO:IVO + 1],
                                                                         in1=res_i[:, i % 2, :], op0=ALU.mult, op1=ALU.add))
                    misc.readers[k] = [t["sum", i]]
                    wait(nc.sync, t["sum", i])
                    t["stored", i] = load(f"out{i % 2}", out[ds(blk * BLK + i * P, P), :], out_o[:, i % 2, :])
                return fill, empty

            units = [(None, lambda k: divisors()), (None, None), (None, None), (None, lambda k: divide(0)), tile(0), tile(1),
                     (None, lambda k: divide(1)), (None, None), tile(2), tile(3)]
            L["units"] += [(f, g, t) for f, g in units]

        def run_units(L):
            before = L["waiting"].pop() if L["waiting"] else None
            fill, empty, t = L["units"].pop(0) if L["units"] else (None, None, None)
            if fill:
                fill()
            if before:
                before[0](before[1])
            if fill:
                L["waiting"].append((empty, t["bank"]))
            elif empty:
                empty(None)

        def load_stack(i, group):
            batch, g = group // KC, group % KC
            name = f"stack{i}"
            for half in range(2):
                blk = batch * 2 + half
                cols = slice(half * HALF, (half + 1) * HALF)
                src = lambda k: feat_d[k][ds(blk * DM + g * P, P), :].rearrange("(h p) n -> p h n", p=HD)
                norm = lambda s: aug_d[s][ds(blk * P + g * G4 * AUG, G4 * AUG), :].rearrange("(h p) n -> p h n", p=AUG)
                for r, (kq, kk) in enumerate((("qh", "kh"), ("qh", "kl"), ("ql", "kh"))):
                    load(name, QS[i][r * HD:(r + 1) * HD, :, cols], src(kq))
                    load(name, KS[i][r * HD:(r + 1) * HD, :, cols], src(kk))
                load(name, QS[i][3 * HD:ROWS, :, cols], norm("q"))
                load(name, KS[i][3 * HD:ROWS, :, cols], norm("k"))
            return load(name, VS[i][:, :, :], v_d[ds(batch * N, N), ds(g * P, P)].rearrange("(j p) d -> p j d", p=P))

        def attention(m, blk_in, blk_out, prefetch):
            misc, L = Misc(), {"units": [], "waiting": []}
            ready = [None, load_stack(1, m * 2 + 1)]
            if blk_in is not None:
                projections(blk_in, misc, L)
            if blk_out is not None:
                output(blk_out, misc, L)
            QUADS = 2 * 2 * JC
            SLOTS = 2 * (QUADS + 3)
            n_units, used = len(L["units"]), 0
            QK, CL, SQ, RT, WP, WD, PV, OZ = {}, {}, {}, {}, {}, {}, {}, {}
            stored = None

            def distances(t):
                q, pair = t // 2, t % 2
                gi, half, j = q // (2 * JC), q // JC % 2, q % JC
                wait(nc.tensor, CL.get(t - 2), ready[gi] if q % (2 * JC) == 0 and pair == 0 else None)
                for h in (2 * pair, 2 * pair + 1):
                    col = (t % 2) * 2 * HALF + (h % 2) * HALF
                    mm = nc.tensor.matmul(pU[:, col:col + HALF], KS[gi][:, h, j * P:(j + 1) * P],
                                          QS[gi][:, h, half * HALF:(half + 1) * HALF], start=True, stop=True)
                QK[t] = PE.done(mm)
                wait(nc.vector, QK[t], PV.get(q - 4))
                cols = slice(pair * 2 * HALF, (pair + 1) * 2 * HALF)
                CL[t] = DV.done(nc.vector.tensor_scalar(cosh[:, q % 4, cols], pU[:, cols], CS, None, ALU.max))

            def square(q):
                wait(nc.scalar, CL[2 * q + 1], WP.get(q - 3), WD.get(q - 3))
                SQ[q] = AC.done(nc.scalar.activation(root[:, q % 3, :], cosh[:, q % 4, :], ACT.Square))

            def sinh(q):
                wait(nc.scalar, SQ[q])
                RT[q] = AC.done(nc.scalar.activation(root[:, q % 3, :], root[:, q % 3, :], ACT.Sqrt, bias=-CS * CS))

            def weights_pool(q):
                c = slice(0, POOL_COLS)
                wait(nc.gpsimd, RT[q])
                WP[q] = PL.done(nc.gpsimd.tensor_tensor(cosh[:, q % 4, c], cosh[:, q % 4, c], root[:, q % 3, c], ALU.subtract))

            def weights_dve(q):
                c = slice(POOL_COLS, G4 * HALF)
                wait(nc.vector, RT[q])
                WD[q] = DV.done(nc.vector.tensor_tensor(cosh[:, q % 4, c], cosh[:, q % 4, c], root[:, q % 3, c], ALU.subtract))

            def sums(q):
                nonlocal stored
                gi, half, j = q // (2 * JC), q // JC % 2, q % JC
                wait(nc.tensor, WP[q], WD[q], OZ.get(q // JC - 1) if j == 0 else None)
                for h in range(G4):
                    nc.tensor.matmul(pO[h * HD:(h + 1) * HD, :], VS[gi][:, j, h * HD:(h + 1) * HD],
                                     cosh[:, q % 4, h * HALF:(h + 1) * HALF], start=j == 0, stop=j == JC - 1)
                for h in range(G4):
                    mm = nc.tensor.matmul(pZ[h * HD:(h + 1) * HD, :], ones[:, :],
                                          cosh[:, q % 4, h * HALF:(h + 1) * HALF], start=j == 0, stop=j == JC - 1)
                PV[q] = PE.done(mm)
                if j == JC - 1:
                    wait(nc.scalar, PV[q], stored)
                    AC.done(nc.scalar.copy(o_s[:, :], pO[:, :]))
                    r = OZ[q // JC] = AC.done(nc.scalar.copy(z_s[:, :], pZ[:, :]))
                    group = m * 2 + gi
                    batch, g = group // KC, group % KC
                    blk = batch * 2 + half
                    wait(nc.sync, r)
                    load("att", att_d[ds(blk * DM + g * P, P), :], o_s[:, :])
                    stored = load("att", z_d[ds(blk * H + g * G4, G4), :], z_s[0:P:HD, :])

            for s in range(SLOTS):
                q = s // 2
                if s < 2 * QUADS:
                    distances(s)
                if s % 2:
                    if q < QUADS:
                        square(q)
                    if 0 <= q - 1 < QUADS:
                        sinh(q - 1)
                        weights_pool(q - 1)
                else:
                    if 0 <= q - 2 < QUADS:
                        weights_dve(q - 2)
                    if 0 <= q - 3 < QUADS:
                        sums(q - 3)
                if s == 2 * (2 * JC) + 2 and prefetch:
                    wait(nc.sync, PV[QUADS // 2 - 3], QK[2 * (2 * JC) - 1])
                while used < n_units and used * SLOTS < (s + 1) * n_units * 1.06:
                    run_units(L)
                    used += 1
            weights_dve(QUADS - 1) if QUADS - 1 not in WD else None
            for q in range(QUADS - 3, QUADS):
                if q not in PV:
                    sums(q)
            while L["units"] or L["waiting"]:
                run_units(L)
            if prefetch:
                wait(nc.sync, (PE.sem, PE.count))
                load_stack(0, m * 2 + 2)
            meet()

        def units_only(blk_in=None, blk_out=None):
            misc, L = Misc(), {"units": [], "waiting": []}
            if blk_in is not None:
                projections(blk_in, misc, L)
            if blk_out is not None:
                output(blk_out, misc, L)
            while L["units"] or L["waiting"]:
                run_units(L)
            meet()

        LOOPS = B * KC // 2
        with nc.Fori(0, LEAD) as m:
            units_only(blk_in=m)
        load_stack(0, 0)
        meet()
        with nc.Fori(0, LATE) as m:
            attention(m, m + LEAD, None, True)
        with nc.Fori(LATE, LOOPS - LEAD) as m:
            attention(m, m + LEAD, m - LATE, True)
        with nc.Fori(LOOPS - LEAD, LOOPS - 1) as m:
            attention(m, None, m - LATE, True)
        attention(LOOPS - 1, None, LOOPS - 1 - LATE, False)
        with nc.Fori(LOOPS - LATE, LOOPS) as m:
            units_only(blk_out=m)


def general(nc, e):
    S, PE, AC, DV, PL = e["S"], e["PE"], e["AC"], e["DV"], e["PL"]
    meet, load, on_dve = e["meet"], e["load"], e["on_dve"]
    x, out, scale, v_d, res_d = e["x"], e["out"], e["scale"], e["v_d"], e["res_d"]
    IV = e["IV"]
    with ExitStack() as ctx:
        def sb(name, shape, dt=F32):
            return ctx.enter_context(nc.sbuf_tensor(name, shape, dt))

        q_t, k_t, o_t = (nc.dram_tensor(n, [DM, T], F32).ap() for n in ("q_t", "k_t", "o_t"))
        Wq, Wk, Wo = (sb(n, [P, KC, DM]) for n in ("Wq32", "Wk32", "Wo32"))
        idn, ones, two = sb("g_idn", [P, P]), sb("g_ones", [P, P]), sb("g_two", [P, 1])
        t0, t1, t2, t3, t4, t5 = (sb(f"t{i}", [P, DM]) for i in range(6))
        xn_t = sb("g_xn_t", [P, KC, P])
        stats, mv, small = sb("g_stats", [P, 6]), sb("g_mv", [P, 2]), sb("g_small", [P, 8])
        KF, QF = sb("KF", [96, N]), sb("QF", [96, N])
        Kh, sq = sb("Kh", [HD, N]), sb("sq", [HD, 2, N])
        Vh = sb("Vh", [P, JC, HD])
        a_b, b_p = sb("a_b", [P, N]), sb("b_p", [P, JC])
        o_sb = sb("o_sb", [HD, N])
        pA, pB, pC, pD, pE = (ctx.enter_context(nc.psum_tensor(f"g_p{n}", [P, HALF], F32)) for n in range(5))

        for dst, src in ((Wq, e["wq_t"]), (Wk, e["wk_t"]), (Wo, e["wo_t"])):
            load("load", dst[:, :, :], src.rearrange("(c p) n -> p c n", p=P))
        load("load", idn[:, :], e["ident"])
        DV.done(nc.vector.memset(ones[:, :], 1.0))
        DV.done(nc.vector.memset(two[:, :], 2.0))
        DV.done(nc.vector.memset(KF[:, :], 0.0))
        on_dve(nc.vector.memset(QF[:, :], 0.0))
        DV.done(nc.vector.memset(KF[32:33, :], 1.0))
        DV.done(nc.vector.memset(QF[64:65, :], 1.0))
        meet()

        with nc.Fori(0, NT) as n:
            row = n * P
            wait(nc.vector, load("x", t0[:, :], x[ds(row, P), :]))
            on_dve(nc.vector.bn_stats(stats[:, :], t0[:, :]))
            on_dve(nc.vector.bn_aggr(mv[:, :], stats[:, :]))
            r = DV.done(nc.vector.tensor_scalar(small[:, 0:1], mv[:, 1:2], EPS, None, ALU.add))
            wait(nc.scalar, r)
            r = AC.done(nc.scalar.activation(small[:, 1:2], small[:, 0:1], ACT.Sqrt))
            wait(nc.vector, r)
            on_dve(nc.vector.reciprocal(small[:, 2:3], small[:, 1:2]))
            on_dve(nc.vector.tensor_scalar(small[:, 3:4], small[:, 0:1], small[:, 2:3], small[:, 2:3], ALU.mult, ALU.mult))
            on_dve(nc.vector.tensor_scalar(small[:, 4:5], small[:, 3:4], -0.5, 1.5, ALU.mult, ALU.add))
            on_dve(nc.vector.tensor_scalar(small[:, 5:6], small[:, 4:5], small[:, 2:3], None, ALU.mult))
            xn = DV.done(nc.vector.tensor_scalar(t1[:, :], t0[:, :], mv[:, 0:1], small[:, 5:6], ALU.subtract, ALU.mult))
            wait(nc.tensor, xn)
            for c in range(KC):
                m = nc.tensor.transpose(pA[:, c * P:(c + 1) * P], t1[:, c * P:(c + 1) * P], idn[:, :])
            wait(nc.vector, PE.done(m))
            xt = DV.done(nc.vector.tensor_copy(xn_t[:, :, :], pA[:, :].rearrange("p (c n) -> p c n", c=KC)))
            wait(nc.tensor, xt)
            for psum, W, hold, dst in ((pB, Wq, t3, q_t), (pC, Wk, t4, k_t)):
                for o in range(KC):
                    for c in range(KC):
                        m = nc.tensor.matmul(psum[:, o * P:(o + 1) * P], W[:, c, o * P:(o + 1) * P], xn_t[:, c, :],
                                             start=c == 0, stop=c == KC - 1)
                wait(nc.vector, PE.done(m))
                r = DV.done(nc.vector.tensor_copy(hold[:, :], psum[:, :]))
                wait(nc.sync, r)
                load("out0", dst.rearrange("(c p) n -> p c n", p=P)[:, :, ds(row, P)],
                     hold[:, :].rearrange("p (c n) -> p c n", c=KC))
            meet()

        with nc.Fori(0, B) as bi:
            with nc.Fori(0, H) as h:
                col, feat = bi * N, h * HD
                load("load", Kh[:, :], k_t[ds(feat, HD), ds(col, N)])
                load("load", QF[0:HD, :], q_t[ds(feat, HD), ds(col, N)])
                ld = load("load", Vh[:, :, :], v_d[ds(col, N), ds(feat, HD)].rearrange("(j p) d -> p j d", p=P))
                wait(nc.vector, ld)
                DV.done(nc.vector.tensor_scalar(KF[0:HD, :], Kh[:, :], -2.0, None, ALU.mult))
                DV.done(nc.vector.tensor_tensor(sq[:, 0, :], Kh[:, :], Kh[:, :], ALU.mult))
                s = DV.done(nc.vector.tensor_tensor(sq[:, 1, :], QF[0:HD, :], QF[0:HD, :], ALU.mult))
                wait(nc.tensor, s)
                for i in range(2):
                    cols = slice(i * HALF, (i + 1) * HALF)
                    nc.tensor.matmul(pA[32:64, :], ones[0:HD, 0:32], sq[:, 1, cols], start=True, stop=True)
                    nc.tensor.matmul(pA[64:96, :], ones[0:HD, 0:32], sq[:, 0, cols], start=True, stop=True)
                    m = PE.done(nc.tensor.matmul(pB[:, :], ones[0:HD, :], sq[:, 1, cols], start=True, stop=True))
                    wait(nc.vector, m)
                    DV.done(nc.vector.tensor_copy(QF[32:33, cols], pA[32:33, :]))
                    DV.done(nc.vector.tensor_copy(KF[64:65, cols], pA[64:65, :]))
                    s = DV.done(nc.vector.tensor_scalar(a_b[:, cols], pB[:, :], -1.0, 1.0, ALU.mult, ALU.add))
                    wait(nc.tensor, s)
                for j in range(JC):
                    m = nc.tensor.matmul(pC[:, j:j + 1], sq[:, 0, j * P:(j + 1) * P], ones[0:HD, 0:1], start=True, stop=True)
                wait(nc.vector, PE.done(m))
                on_dve(nc.vector.tensor_scalar(b_p[:, :], pC[:, 0:JC], -1.0, 1.0, ALU.mult, ALU.add))
                for i in range(2):
                    cols = slice(i * HALF, (i + 1) * HALF)
                    for j in range(JC):
                        m = PE.done(nc.tensor.matmul(pA[:, :], KF[:, j * P:(j + 1) * P], QF[:, cols], start=True, stop=True))
                        on_dve(nc.vector.tensor_scalar(t0[:, :], a_b[:, cols], b_p[:, j:j + 1], 1e-6, ALU.mult, ALU.max))
                        on_dve(nc.vector.reciprocal(t1[:, :], t0[:, :]))
                        wait(nc.vector, m)
                        u = DV.done(nc.vector.scalar_tensor_tensor(out=t2[:, :], in0=pA[:, :], scalar=0.0, in1=t1[:, :], op0=ALU.max, op1=ALU.mult))
                        wait(nc.scalar, u)
                        AC.done(nc.scalar.activation(t3[:, :], t2[:, :], ACT.Sqrt, scale=2.0))
                        s = AC.done(nc.scalar.activation(t4[:, :], t2[:, :], ACT.Sqrt, scale=2.0, bias=two[:, 0:1]))
                        wait(nc.vector, s)
                        on_dve(nc.vector.tensor_tensor(t5[:, :], t3[:, :], t4[:, :], ALU.mult))
                        on_dve(nc.vector.scalar_tensor_tensor(out=t0[:, :], in0=t2[:, :], scalar=2.0, in1=t5[:, :], op0=ALU.mult, op1=ALU.add))
                        on_dve(nc.vector.tensor_scalar(t1[:, :], t0[:, :], 1.0, None, ALU.add))
                        w = DV.done(nc.vector.reciprocal(t0[:, :], t1[:, :]))
                        wait(nc.tensor, w)
                        nc.tensor.matmul(pD[0:HD, :], Vh[:, j, :], t0[:, :], start=j == 0, stop=j == JC - 1)
                        m = PE.done(nc.tensor.matmul(pE[0:HD, :], ones[:, 0:HD], t0[:, :], start=j == 0, stop=j == JC - 1))
                        wait(nc.vector, m)
                    on_dve(nc.vector.reciprocal(t1[0:HD, :], pE[0:HD, :]))
                    s = on_dve(nc.vector.tensor_tensor(o_sb[:, cols], pD[0:HD, :], t1[0:HD, :], ALU.mult))
                    wait(nc.tensor, s)
                wait(nc.sync, s)
                load("out0", o_t[ds(feat, HD), ds(col, N)], o_sb[:, :])
                meet()

        with nc.Fori(0, NT) as n:
            row = n * P
            load("load", xn_t[:, :, :], o_t.rearrange("(c p) n -> p c n", p=P)[:, :, ds(row, P)])
            ld = load("load", t0[:, :], res_d[ds(row, P), :])
            wait(nc.tensor, ld)
            for c in range(KC):
                m = nc.tensor.matmul(pA[:, :], xn_t[:, c, :], Wo[:, c, :], start=c == 0, stop=c == KC - 1)
            wait(nc.vector, PE.done(m), ld)
            s = DV.done(nc.vector.scalar_tensor_tensor(out=t1[:, :], in0=pA[:, :], scalar=scale[:, IV:IV + 1], in1=t0[:, :],
                                                       op0=ALU.mult, op1=ALU.add))
            wait(nc.sync, s)
            load("out0", out[ds(row, P), :], t1[:, :])
            meet()


def kernel(L0_attn_x, L0_attn_Wq, L0_attn_Wk, L0_attn_Wv, L0_attn_Wo, L0_ffn_kernel, L0_ffn_bias, L0_ffn_a, L0_ffn_b):
    import numpy as np
    import concourse.bacc as bacc
    from concourse.bass_utils import run_bass_kernel_spmd

    lay = np.ascontiguousarray
    arrays = {
        "x": lay(np.asarray(L0_attn_x).reshape(T, DM)),
        "wq_t": lay(np.asarray(L0_attn_Wq).T), "wk_t": lay(np.asarray(L0_attn_Wk).T),
        "wv_t": lay(np.asarray(L0_attn_Wv).T), "wo_t": lay(np.asarray(L0_attn_Wo).T),
        "ffn_w": lay(L0_ffn_kernel),
        "bias": lay(np.broadcast_to(np.asarray(L0_ffn_bias), (P, DM))),
        "a_t": lay(np.asarray(L0_ffn_a).T), "b": lay(L0_ffn_b),
        "ident": np.eye(P, dtype=np.float32),
    }
    nc = bacc.Bacc("TRN2", target_bir_lowering=False, num_devices=1)
    args = {k: nc.dram_tensor(f"in_{k}", a.shape, F32, kind="ExternalInput").ap() for k, a in arrays.items()}
    out = nc.dram_tensor("out_0", (T, DM), F32, kind="ExternalOutput").ap()
    build(nc, out=out, **args)
    r = run_bass_kernel_spmd(nc, [{f"in_{k}": a for k, a in arrays.items()}], core_ids=[0])
    return r.results[0]["out_0"].reshape(B, N, DM)
```

```python
import concourse.bass as bass
from concourse import mybir
from contextlib import ExitStack

F32, F16, I32 = mybir.dt.float32, mybir.dt.float16, mybir.dt.int32
ALU = mybir.AluOpType
ACT = mybir.ActivationFunctionType
AX = mybir.AxisListType
ds = bass.ds

B, N, DM, H = 8, 1024, 512, 16
HD = DM // H
P = 128
T = B * N
KC = DM // P
G4 = P // HD
NT = T // P
JC = N // P
HALF = 512
BLK = 512
TPB = BLK // P
NB = T // BLK
RANK = 16
EPS = 1e-5
ROUND = 1.5 * 2.0 ** 23
AUG = 8
ROWS = 3 * HD + AUG
RS = 64.0
CS = RS * RS / 2
NORM_MIN = 16.0
W_TOP = 16.0
LEAD = 2
LATE = 2
RING = 4
QUADS = 2 * 2 * JC
TILES = 2 * QUADS
HANDOVER = 8
PREFETCH = 40
CLEARED = 10
BUDGET = 6, 7
FOLD, NEXT_HEAD = 12, 36
HEAD = 2
OUT_FIRST, OUT_STEP = 8, 3
UNIT_TRANSFERS = "x", "feat", "v", "res", "z", "rz", "raw", "resin0", "resin1", "out0", "out1"
POOL_COLS = 1664


class Signals:

    def __init__(self, sem):
        self.sem, self.count = sem, 0

    def done(self, ins, by=1):
        ins.then_inc(self.sem, by)
        self.count += by
        return self.sem, self.count


class Current:

    def __init__(self, signals, name):
        self.signals, self.name = signals, name

    def done(self, ins):
        return self.signals[self.name].done(ins)

    def all(self):
        s = self.signals[self.name]
        return s.sem, s.count


class Buffers:

    def __init__(self, zc, raw, rzb, ah, al, res_i):
        self.zc, self.raw, self.rzb, self.ah, self.al, self.res_i = zc, raw, rzb, ah, al, res_i


class Tickets(dict):

    def __init__(self, before=None):
        super().__init__()
        self.before = before

    def get(self, key, default=None):
        if key in self or self.before is None:
            return super().get(key, default)
        if isinstance(key, tuple):
            return self.before.get(key[:-1] + (key[-1] + TPB,)) if key[-1] < 0 else default
        return self.before.get(key)


def wait(engine, *tickets):
    for t in tickets:
        if t is not None:
            engine.wait_ge(*t)


def build(nc, x, wq_t, wk_t, wv_t, wo_t, ffn_w, bias, a_t, b, ident, out):
    ctx = ExitStack()
    with ctx:
        engines = ("pe", "act", "dve", "pool")
        transfers = ("load", "Wf", "Wq", "Wk", "Wv", "Wo", "x", "x1", "feat", "v", "res", "z", "rz", "raw", "resin0", "resin1", "out0", "out1",
                     "z+", "rz+", "raw+", "resin0+", "resin1+", "out0+", "out1+")
        stages = ("QK", "CL", "SQ", "RT", "WP", "WD", "PV", "OZ", "att", "stack0a", "stack0b", "stack1", "met", "clear")
        semaphore = lambda n: ctx.enter_context(nc.semaphore("s_" + n))
        sets = [{n: Signals(semaphore(f"{n}_{i}")) for n in engines + transfers} for i in range(2)]
        stage_sems = [{n: semaphore(f"{n}_{i}") for n in stages} for i in range(2)]
        S = dict(sets[0])
        current = {n: Current(S, n) for n in engines}
        PE, AC, DV, PL = (current[n] for n in engines)

        def use(i):
            S.update(sets[i])
            for s in S.values():
                s.count = 0

        def meet():
            for n in transfers:
                if S[n].count:
                    nc.sync.wait_ge(S[n].sem, S[n].count)
            nc.all_engine_barrier()
            for s in S.values():
                if s.count:
                    nc.sync.sem_clear(s.sem)
                s.count = 0
            nc.all_engine_barrier()

        def load(name, dst, src):
            return S[name].done(nc.sync.dma_start(dst, src), 16)

        def on_dve(ins):
            t = DV.done(ins)
            wait(nc.vector, t)
            return t

        def scratch(name, shape, dt):
            return nc.dram_tensor(name, shape, dt).ap()

        feat_d = {k: scratch(f"{k}_d", [NB * DM, BLK], F16) for k in ("qh", "ql", "kh", "kl")}
        aug_d = {k: scratch(f"aug_{k}_d", [NB * P, BLK], F16) for k in "qk"}
        v_d = scratch("v_d", [T, DM], F32)
        res_d = scratch("res_d", [T, DM], F32)
        att_d = scratch("att_d", [NB * DM, BLK], F32)
        z_d = scratch("z_d", [NB * H, BLK], F32)
        rz_d = scratch("rz_d", [NB * H, BLK], F32)

        outer_sb = lambda name, shape, dt=F32: ctx.enter_context(nc.sbuf_tensor(name, shape, dt))
        scale = outer_sb("scale", [P, 16])
        flag = outer_sb("flag", [P, 2 * H])
        flag_all = outer_sb("flag_all", [P, 2])
        flag_int = outer_sb("flag_int", [P, 1], I32)
        IQ, IK, IV, IO, IF, IVO = 5, 6, 7, 8, 9, 10

        env = dict(locals())
        fast(nc, env)

        r = DV.done(nc.vector.tensor_reduce(flag_all[:, 0:1], flag[:, :], AX.X, ALU.max))
        wait(nc.gpsimd, r)
        r = PL.done(nc.gpsimd.partition_all_reduce(flag_all[:, 1:2], flag_all[:, 0:1], P, bass.bass_isa.ReduceOp.max))
        wait(nc.vector, r)
        DV.done(nc.vector.tensor_copy(flag_int[:, :], flag_all[:, 1:2]))
        wait(nc.vector, DV.all())
        meet()
        small_norm = nc.values_load(flag_int[0:1, 0:1], min_val=0, max_val=1)
        with nc.If(small_norm > 0):
            general(nc, env)
        nc.end_ifs()


def fast(nc, e):
    S, PE, AC, DV, PL = e["S"], e["PE"], e["AC"], e["DV"], e["PL"]
    meet, load, on_dve = e["meet"], e["load"], e["on_dve"]
    feat_d, aug_d, v_d, res_d, att_d, z_d, rz_d = (e[k] for k in ("feat_d", "aug_d", "v_d", "res_d", "att_d", "z_d", "rz_d"))
    x, out, scale, flag = e["x"], e["out"], e["scale"], e["flag"]
    use, sets, stage_sems, transfers, engines = (e[k] for k in ("use", "sets", "stage_sems", "transfers", "engines"))
    IQ, IK, IV, IO, IF, IVO = (e[k] for k in ("IQ", "IK", "IV", "IO", "IF", "IVO"))
    with ExitStack() as ctx:
        def sb(name, shape, dt=F32):
            return ctx.enter_context(nc.sbuf_tensor(name, shape, dt))

        def ps(name, cols=HALF):
            return ctx.enter_context(nc.psum_tensor(name, [P, cols], F32))

        W = {k: (sb(f"W{k}h", [P, KC, DM], F16), sb(f"W{k}l", [P, KC, DM], F16)) for k in "qkvof"}
        bias_b, idn, idn16, ones = sb("bias_b", [P, DM]), sb("idn", [P, P]), sb("idn16", [P, P], F16), sb("ones", [P, HD])
        QS = [sb(f"QS{i}", [ROWS, G4, N], F16) for i in range(2)]
        KS = [sb(f"KS{i}", [ROWS, G4, N], F16) for i in range(2)]
        VS = [sb(f"VS{i}", [P, JC, P]) for i in range(2)]
        cosh = sb("cosh", [P, RING, G4 * HALF])
        root = sb("root", [P, RING, G4 * HALF])
        xt = sb("xt", [P, TPB, DM])
        xn = sb("xn", [P, 2, DM])
        xh, xl = sb("xh", [P, 2, KC, P], F16), sb("xl", [P, 2, KC, P], F16)
        qk = sb("qk", [P, 2, DM])
        sqr = sb("sqr", [P, 2, DM])
        aug = sb("aug", [P, 2, H, AUG], F16)
        feat = {k: sb(f"feat_{k}", [P, KC, 2 * P], F16) for k in ("qh", "ql", "kh", "kl")}
        aug_o = sb("aug_o", [P, 2, 2 * P], F16)
        v_o, f_o = sb("v_o", [P, DM]), sb("f_o", [P, DM])
        stats, mv, ln = sb("stats", [P, TPB, 6]), sb("mv", [P, TPB, 2]), sb("ln", [P, 5, TPB])
        nrm, rcp = sb("nrm", [P, 2, H]), sb("rcp", [P, 3, 2, H])
        o_s, z_s = sb("o_s", [P, HALF]), sb("z_s", [P, HALF])
        raw, rzb = sb("raw", [P, KC, 2 * P]), sb("rzb", [P, KC, 2 * P])
        zc = sb("zc", [P, 2, BLK * H // P])
        ah, al = sb("ah", [P, KC, 2 * P], F16), sb("al", [P, KC, 2 * P], F16)
        res_i = sb("res_i", [P, 2, DM])
        buffers = Buffers(zc, raw, rzb, ah, al, res_i)
        pU = ps("pU", 4 * HALF)
        pO, pZ = ps("pO"), ps("pZ")
        pM = [ps("pM0"), ps("pM1")]

        W32 = {k: cosh[:, i, :].rearrange("p (c n) -> p c n", c=KC) for i, k in enumerate("qkvo")}
        W32["f"] = root[:, 0, :].rearrange("p (c n) -> p c n", c=KC)
        tmp = root[:, 1, :].rearrange("p (c n) -> p c n", c=KC)
        At, Bl = root[0:RANK, 2, 0:DM], root[0:RANK, 2, DM:2 * DM]
        xt1 = root[:, 3, :].rearrange("p (i n) -> p i n", i=TPB)
        arrived = {}
        for k, src in zip("fqkvo", (e["ffn_w"], e["wq_t"], e["wk_t"], e["wv_t"], e["wo_t"])):
            arrived[k] = load("W" + k, W32[k], src.rearrange("(c p) n -> p c n", p=P))
        load("load", At, e["a_t"])
        load("load", Bl, e["b"])
        load("load", bias_b[:, :], e["bias"])
        loaded = load("load", idn[:, :], e["ident"])
        tokens = [load(name, dst, x[blk * BLK:(blk + 1) * BLK, :].rearrange("(i p) n -> p i n", p=P))
                  for name, dst, blk in (("x", xt[:, :, :], 0), ("x1", xt1, 1))]
        DV.done(nc.vector.memset(ones[:, :], 1.0))
        DV.done(nc.vector.memset(flag[:, :], 0.0))
        on_dve(nc.vector.memset(aug[:, :, :, :], 0.0))
        DV.done(nc.vector.memset(aug[:, 0, :, 6:7], RS))
        DV.done(nc.vector.memset(aug[:, 1, :, 6:7], CS / RS))
        top = sb("top", [P, 12])
        topi = top[:, :].bitcast(I32)

        def largest(k, col):
            return DV.done(nc.vector.tensor_reduce(top[:, col:col + 1], W32[k], AX.XY, ALU.max, apply_absolute_value=True))

        def everywhere(dst, cols, ready):
            wait(nc.gpsimd, ready)
            return PL.done(nc.gpsimd.partition_all_reduce(dst, top[:, cols], P, bass.bass_isa.ReduceOp.max))

        def scales(c):
            t, inverse = slice(4 + c.start, 4 + c.stop), slice(IQ + c.start, IQ + c.stop)
            on_dve(nc.vector.tensor_scalar(top[:, t], scale[:, c], 2.0 ** -100, 2.0 ** 100, ALU.max, ALU.min))
            on_dve(nc.vector.tensor_scalar(topi[:, t], topi[:, t], 0x7F800000, None, ALU.bitwise_and))
            on_dve(nc.vector.tensor_scalar(scale[:, inverse], top[:, t], 1.0 / W_TOP, None, ALU.mult))
            return on_dve(nc.vector.reciprocal(scale[:, c], scale[:, inverse]))

        def split(k, i, scaled):
            wait(nc.scalar, scaled)
            high = AC.done(nc.scalar.activation(W[k][0][:, :, :], W32[k], ACT.Copy, scale=scale[:, i:i + 1]))
            wait(nc.vector, high)
            return DV.done(nc.vector.scalar_tensor_tensor(out=W[k][1][:, :, :], in0=W32[k], scalar=scale[:, i:i + 1], in1=W[k][0][:, :, :],
                                                   op0=ALU.mult, op1=ALU.subtract))

        wait(nc.vector, arrived["f"])
        all_f = everywhere(top[:, 1:2], slice(0, 1), largest("f", 0))
        for i, k in enumerate("qkvo"):
            wait(nc.vector, arrived[k])
            r = largest(k, 4 + i)
        all_w = everywhere(scale[:, 0:4], slice(4, 8), r)
        wait(nc.gpsimd, loaded)
        wait(nc.vector, loaded)
        DV.done(nc.vector.tensor_copy(idn16[:, :], idn[:, :]))
        wait(nc.tensor, loaded)
        for c in range(KC):
            low_rank = PE.done(nc.tensor.matmul(pU[:, c * DM:(c + 1) * DM], At[:, c * P:(c + 1) * P], Bl, start=True, stop=True))
        wait(nc.vector, all_w)
        scaled = scales(slice(0, 4))
        weights = {k: split(k, i, scaled) for i, k in enumerate("qkv")}

        def fold():
            wait(nc.vector, all_f)
            on_dve(nc.vector.tensor_scalar(top[:, 2:3], top[:, 1:2], 1.0 / 7.0, None, ALU.mult))
            on_dve(nc.vector.reciprocal(top[:, 3:4], top[:, 2:3]))
            on_dve(nc.vector.tensor_scalar(tmp, W32["f"], top[:, 3:4], ROUND, ALU.mult, ALU.add))
            on_dve(nc.vector.tensor_scalar(tmp, tmp, ROUND, -8.0, ALU.subtract, ALU.max))
            on_dve(nc.vector.tensor_scalar(tmp, tmp, 7.0, top[:, 2:3], ALU.min, ALU.mult))
            wait(nc.vector, low_rank)
            on_dve(nc.vector.tensor_tensor(W32["f"], pU[:, :].rearrange("p (c n) -> p c n", c=KC), tmp, ALU.add))
            weights["all f"] = everywhere(scale[:, 4:5], slice(8, 9), largest("f", 8))

        def split_f():
            wait(nc.vector, weights["all f"])
            weights["f"] = split("f", 4, scales(slice(4, 5)))

        def split_o():
            weights["o"] = split("o", 3, scaled)
            on_dve(nc.vector.tensor_tensor(scale[:, IVO:IVO + 1], scale[:, IV:IV + 1], scale[:, IO:IO + 1], ALU.mult))


        class Misc:

            def __init__(self):
                self.n, self.readers = 0, [[], []]

            def bank(self, ready):
                while self.readers[self.n % 2] is None or not ready():
                    yield None
                i = self.n % 2
                self.n += 1
                wait(nc.tensor, *self.readers[i])
                self.readers[i] = None
                return i

        def product(bank, hi, lo, w):
            for c in range(KC):
                wh, wl = w[0][:, c, :], w[1][:, c, :]
                nc.tensor.matmul(bank[:, :], hi(c), wh, start=c == 0, stop=False)
                nc.tensor.matmul(bank[:, :], hi(c), wl, start=False, stop=False)
                last = nc.tensor.matmul(bank[:, :], lo(c), wh, start=False, stop=c == KC - 1)
                yield 3
            return PE.done(last)

        def load_x(blk):
            return load("x", xt[:, :, :], x[ds(blk * BLK, BLK), :].rearrange("(i p) n -> p i n", p=P))

        def projections(blk, misc, loaded_x, xt=xt, next_blk=None, before=None):
            t = Tickets(before)
            t["x"] = loaded_x

            def moments(i):
                wait(nc.vector, t["x"])
                t["stats"] = DV.done(nc.vector.bn_stats(stats[:, i, :], xt[:, i, :]))

            def variance():
                wait(nc.vector, t["stats"])
                for i in range(TPB):
                    r = DV.done(nc.vector.bn_aggr(mv[:, i, :], stats[:, i, :]))
                wait(nc.vector, r)
                r = DV.done(nc.vector.tensor_scalar(ln[:, 0, :], mv[:, :, 1], EPS, None, ALU.add))
                wait(nc.scalar, r)
                t["std"] = AC.done(nc.scalar.activation(ln[:, 1, :], ln[:, 0, :], ACT.Sqrt))

            def inverse():
                wait(nc.vector, t["std"])
                on_dve(nc.vector.reciprocal(ln[:, 2, :], ln[:, 1, :]))
                on_dve(nc.vector.tensor_tensor(ln[:, 3, :], ln[:, 2, :], ln[:, 2, :], ALU.mult))
                on_dve(nc.vector.tensor_tensor(ln[:, 4, :], ln[:, 3, :], ln[:, 0, :], ALU.mult))
                on_dve(nc.vector.tensor_scalar(ln[:, 3, :], ln[:, 4, :], -0.5, 1.5, ALU.mult, ALU.add))
                on_dve(nc.vector.tensor_tensor(ln[:, 1, :], ln[:, 2, :], ln[:, 3, :], ALU.mult))

            def normalise(i):
                wait(nc.vector, t.get(("T", i - 2)))
                t["xn", i] = DV.done(nc.vector.tensor_scalar(xn[:, i % 2, :], xt[:, i, :], mv[:, i, 0:1], ln[:, 1, i:i + 1],
                                                             ALU.subtract, ALU.mult))
                wait(nc.gpsimd, t["xn", i])
                t["xb", i] = PL.done(nc.gpsimd.tensor_tensor(xt[:, i, :], xt[:, i, :], bias_b[:, :], ALU.add))

            def transposes(i):
                def fill():
                    k = t["bank", "T", i] = yield from misc.bank(lambda: ("xn", i) in t)
                    wait(nc.tensor, t["xn", i])
                    for c in range(KC):
                        m = nc.tensor.transpose(pM[k][:, c * P:(c + 1) * P], xn[:, i % 2, c * P:(c + 1) * P], idn[:, :])
                        yield 1
                    t["T", i] = PE.done(m)

                def empty():
                    k = t["bank", "T", i]
                    v = pM[k][:, :].rearrange("p (c n) -> p c n", c=KC)
                    wait(nc.vector, t["T", i], t.get(("F", i - 2)))
                    on_dve(nc.vector.tensor_copy(xh[:, i % 2, :, :], v))
                    t["xT", i] = DV.done(nc.vector.tensor_tensor(xl[:, i % 2, :, :], v, xh[:, i % 2, :, :], ALU.subtract))
                    misc.readers[k] = [t["xT", i]]
                return fill, [(1, empty)] + ([(2, lambda: normalise(i + 2))] if i + 2 < TPB else [])

            def unit(i, key):
                def fill():
                    k = t["bank", key, i] = yield from misc.bank(lambda: ("xT", i) in t and key in weights)
                    wait(nc.tensor, t["xT", i], weights[key])
                    t[key.upper(), i] = yield from product(pM[k], lambda c: xh[:, i % 2, c, :], lambda c: xl[:, i % 2, c, :], W[key])
                return fill

            def qk_unit(i, s):
                key = "qk"[s]

                def empty():
                    k = t["bank", key, i]
                    wait(nc.scalar, t[key.upper(), i], t.get(("TX", s, i - 1)), t.get(("sum", s, i - 1)))
                    r = AC.done(nc.scalar.activation(qk[:, s, :], pM[k][:, :], ACT.Copy, scale=scale[:, IQ + s:IQ + s + 1]))
                    misc.readers[k] = [r]
                    wait(nc.scalar, r)
                    t["sq", s, i] = AC.done(nc.scalar.activation(sqr[:, s, :], qk[:, s, :], ACT.Square))

                def norm():
                    wait(nc.vector, t["sq", s, i], t.get(("augd", i - 1)))
                    t["sum", s, i] = DV.done(nc.vector.tensor_reduce(nrm[:, s, :], sqr[:, s, :].rearrange("p (h d) -> p h d", h=H), AX.X, ALU.add))
                more = [(2, lambda: factors(i)), (3, lambda: scaled(i)), (4, lambda: aug_rows(i))] if s == 1 else []
                return unit(i, key), [(1, empty), (2, norm)] + more

            def factors(i):
                wait(nc.vector, t["sum", 1, i])
                fl = flag[:, :].rearrange("p (s h) -> p s h", s=2)
                DV.done(nc.vector.scalar_tensor_tensor(out=fl, in0=nrm[:, :, :], scalar=NORM_MIN, in1=fl, op0=ALU.is_lt, op1=ALU.max))
                on_dve(nc.vector.tensor_scalar(rcp[:, 0, :, :], nrm[:, :, :], NORM_MIN, 1.0, ALU.max, ALU.subtract))
                on_dve(nc.vector.reciprocal(rcp[:, 1, :, :], rcp[:, 0, :, :]))
                on_dve(nc.vector.tensor_tensor(rcp[:, 2, :, :], nrm[:, :, :], rcp[:, 1, :, :], ALU.mult))

            def scaled(i):
                R, M = rcp[:, 1, :, :], rcp[:, 2, :, :]
                v = qk[:, :, :].rearrange("p s (h d) -> p s h d", h=H)
                for s, factor in ((0, -2.0 * RS), (1, RS)):
                    t["scaled", i] = DV.done(nc.vector.scalar_tensor_tensor(
                        out=v[:, s], in0=v[:, s], scalar=factor, in1=R[:, s, :].unsqueeze(2).to_broadcast([P, H, HD]),
                        op0=ALU.mult, op1=ALU.mult))

            def aug_rows(i):
                R, M = rcp[:, 1, :, :], rcp[:, 2, :, :]
                wait(nc.vector, t.get(("AU", i - 1)))
                two = lambda a: a.unsqueeze(2).to_broadcast([P, H, 2])
                q, k = aug[:, 0, :, :], aug[:, 1, :, :]
                for dst, full in ((q[:, :, 0:2], M[:, 0, :]), (q[:, :, 3:5], R[:, 0, :]), (k[:, :, 0:3:2], R[:, 1, :]), (k[:, :, 3:6:2], M[:, 1, :])):
                    r = DV.done(nc.vector.tensor_scalar(dst, two(full), RS, None, ALU.mult))
                wait(nc.vector, r)
                for dst, full, high in ((q[:, :, 2], M[:, 0, :], q[:, :, 0]), (q[:, :, 5], R[:, 0, :], q[:, :, 3]),
                                        (k[:, :, 1], R[:, 1, :], k[:, :, 0]), (k[:, :, 4], M[:, 1, :], k[:, :, 3])):
                    r = DV.done(nc.vector.scalar_tensor_tensor(out=dst, in0=full, scalar=RS, in1=high, op0=ALU.mult, op1=ALU.subtract))
                t["augd", i] = r

            def v_unit(i):
                def empty():
                    k = t["bank", "v", i]
                    wait(nc.scalar, t["V", i], t.get("v_stored"))
                    r = AC.done(nc.scalar.copy(v_o[:, :], pM[k][:, :]))
                    misc.readers[k] = [r]
                    wait(nc.sync, r)
                    t["v_stored"] = load("v", v_d[ds(blk * BLK + i * P, P), :], v_o[:, :])
                return unit(i, "v"), [(1, empty)]

            def f_unit(i):
                def empty():
                    k = t["bank", "f", i]
                    wait(nc.vector, t["F", i], t["xb", i], t.get("f_stored"))
                    r = DV.done(nc.vector.scalar_tensor_tensor(out=f_o[:, :], in0=pM[k][:, :], scalar=scale[:, IF:IF + 1],
                                                               in1=xt[:, i, :], op0=ALU.mult, op1=ALU.add))
                    misc.readers[k] = [r]
                    wait(nc.sync, r)
                    t["f_stored"] = load("res", res_d[ds(blk * BLK + i * P, P), :], f_o[:, :])
                    if i == TPB - 1 and next_blk is not None:
                        load_x(next_blk)
                return unit(i, "f"), [(1, empty)]

            def feature_unit(i, s):
                key = "qk"[s]

                def fill():
                    k = t["bank", "X" + key, i] = yield from misc.bank(lambda: ("scaled", i) in t)
                    wait(nc.tensor, t["scaled", i])
                    for c in range(KC):
                        m = nc.tensor.transpose(pM[k][:, c * P:(c + 1) * P], qk[:, s, c * P:(c + 1) * P], idn[:, :])
                        yield 1
                    t["TX", s, i] = PE.done(m)

                def empty():
                    k = t["bank", "X" + key, i]
                    v = pM[k][:, :].rearrange("p (c n) -> p c n", c=KC)
                    cols = slice((i % 2) * P, (i % 2 + 1) * P)
                    fh, fl = feat[key + "h"][:, :, cols], feat[key + "l"][:, :, cols]
                    wait(nc.vector, t["TX", s, i], t.get("feat_stored") if i % 2 == 0 else None)
                    on_dve(nc.vector.tensor_copy(fh, v))
                    t["fl", s, i] = DV.done(nc.vector.tensor_tensor(fl, v, fh, ALU.subtract))
                    misc.readers[k] = [t["fl", s, i]]
                return fill, [(1, empty)]

            def aug_unit(i):
                def fill():
                    k = t["bank", "A", i] = yield from misc.bank(lambda: ("augd", i) in t)
                    wait(nc.tensor, t["augd", i])
                    half = pM[k][:, 0:P].bitcast(F16)
                    for s in range(2):
                        m = nc.tensor.transpose(half[:, s * P:(s + 1) * P], aug[:, s, :, :].rearrange("p h r -> p (h r)"), idn16[:, :])
                    t["AU", i] = PE.done(m)

                def empty():
                    k = t["bank", "A", i]
                    half = pM[k][:, 0:P].bitcast(F16).rearrange("p (s n) -> p s n", s=2)
                    wait(nc.scalar, t["AU", i], t.get("feat_stored") if i % 2 == 0 else None)
                    r = AC.done(nc.scalar.copy(aug_o[:, :, (i % 2) * P:(i % 2 + 1) * P], half))
                    misc.readers[k] = [r]
                    if i % 2:
                        cols = slice((i // 2) * 2 * P, (i // 2 + 1) * 2 * P)
                        wait(nc.sync, r, t["fl", 0, i], t["fl", 1, i])
                        for key, f in feat.items():
                            load("feat", feat_d[key][ds(blk * DM, DM), cols].rearrange("(g p) n -> p g n", p=P), f[:, :, :])
                        for s in range(2):
                            t["feat_stored"] = load("feat", aug_d["qk"[s]][ds(blk * P, P), cols], aug_o[:, s, :])
                return fill, [(1, empty)]

            head = [(n, lambda n=n: moments(n)) for n in range(TPB)] + [(TPB, variance), (TPB + 2, inverse)]
            head += [(TPB + 3, lambda: normalise(0)), (TPB + 4, lambda: normalise(1))]
            units = [transposes(0)]
            for i in range(TPB):
                units += [transposes(i + 1)] if i + 1 < TPB else []
                units += [qk_unit(i, 0), qk_unit(i, 1), v_unit(i), f_unit(i)]
                units += [feature_unit(i, 0), feature_unit(i, 1), aug_unit(i)]
            return head, units, t

        def output(blk, misc, buf, which=""):
            t = {}
            rows = ds(blk * H, H)
            flat = lambda d: d[rows, :].rearrange("r (q n) -> (r q) n", q=P // H)
            t["z"] = load("z" + which, buf.zc[:, 0, :], flat(z_d))

            def divisors():
                wait(nc.vector, t["z"])
                r = DV.done(nc.vector.reciprocal(buf.zc[:, 1, :], buf.zc[:, 0, :]))
                wait(nc.sync, r)
                t["rz"] = load("rz" + which, flat(rz_d), buf.zc[:, 1, :])

            def fetch(i):
                cols = slice(i * 2 * P, (i + 1) * 2 * P)
                wait(nc.sync, t["rz"], t.get(("a", i - 1)))
                load("raw" + which, buf.raw[:, :, :], att_d[ds(blk * DM, DM), cols].rearrange("(g p) n -> p g n", p=P))
                for h in range(G4):
                    src = rz_d[rows, cols].rearrange("(g h) n -> h g n", h=G4)[h:h + 1].to_broadcast([HD, KC, 2 * P])
                    t["raw", i] = load("raw" + which, buf.rzb[h * HD:(h + 1) * HD, :, :], src)

            def divide(i):
                def first():
                    wait(nc.vector, t["raw", i], t.get(("O", 2 * i - 1)))
                    t["divided"] = DV.done(nc.vector.tensor_tensor(buf.raw[:, :, :], buf.raw[:, :, :], buf.rzb[:, :, :], ALU.mult))

                def high():
                    wait(nc.vector, t["divided"])
                    t["high"] = DV.done(nc.vector.tensor_copy(buf.ah[:, :, :], buf.raw[:, :, :]))

                def low():
                    wait(nc.vector, t["high"])
                    t["a", i] = DV.done(nc.vector.tensor_tensor(buf.al[:, :, :], buf.raw[:, :, :], buf.ah[:, :, :], ALU.subtract))
                return [first, high, low]

            def tile(i):
                cols = slice(i % 2 * P, (i % 2 + 1) * P)

                def fill():
                    k = t["bank", i] = yield from misc.bank(lambda: ("a", i // 2) in t)
                    wait(nc.sync, t.get(("stored", i - 2)))
                    t["res", i] = load(f"resin{i % 2}" + which, buf.res_i[:, i % 2, :], res_d[ds(blk * BLK + i * P, P), :])
                    wait(nc.tensor, t["a", i // 2])
                    t["O", i] = yield from product(pM[k], lambda c: buf.ah[:, c, cols], lambda c: buf.al[:, c, cols], W["o"])

                def empty():
                    k = t["bank", i]
                    wait(nc.vector, t["O", i], t["res", i])
                    r = DV.done(nc.vector.scalar_tensor_tensor(out=buf.res_i[:, i % 2, :], in0=pM[k][:, :], scalar=scale[:, IVO:IVO + 1],
                                                               in1=buf.res_i[:, i % 2, :], op0=ALU.mult, op1=ALU.add))
                    misc.readers[k] = [r]
                    wait(nc.sync, r)
                    t["stored", i] = load(f"out{i % 2}" + which, out[ds(blk * BLK + i * P, P), :], buf.res_i[:, i % 2, :])
                more = [(2 + n, f) for n, f in enumerate(divide(1))] if i == 1 else []
                return fill, [(1, empty)] + more

            head = [(0, divisors), (1, lambda: fetch(0))] + [(5 + n, f) for n, f in enumerate(divide(0))] + [(8, lambda: fetch(1))]
            return head, [tile(i) for i in range(TPB)]

        class Schedule:

            def __init__(self, units=()):
                self.parts, self.units, self.left, self.fill = {}, list(units), 0, None

            def at(self, slot, parts):
                for delay, part in parts:
                    self.parts.setdefault(slot + delay, []).append(part)

            def issue(self, slot, budget):
                self.left = min(self.left, 0) + budget
                while self.left > 0 and self.units:
                    if self.fill is None:
                        self.fill = self.units[0][0]()
                    try:
                        cost = next(self.fill)
                    except StopIteration:
                        self.at(slot, self.units.pop(0)[1])
                        self.fill = None
                        continue
                    if cost is None:
                        break
                    self.left -= cost
                for part in self.parts.pop(slot, []):
                    part()

            def finish(self, slot, budget=12):
                while self.parts or self.units:
                    self.issue(slot, budget)
                    slot += 1

        def merge(units, more, first, step):
            units = list(units)
            for n, u in enumerate(more):
                units.insert(first + step * n, u)
            return units

        def load_stack(i, group, half, sem):
            batch, g = group // KC, group % KC

            def fetch(dst, src):
                nc.sync.dma_start(dst, src).then_inc(sem, 16)

            blk = batch * 2 + half
            cols = slice(half * HALF, (half + 1) * HALF)
            src = lambda k: feat_d[k][ds(blk * DM + g * P, P), :].rearrange("(h p) n -> p h n", p=HD)
            norm = lambda s: aug_d[s][ds(blk * P + g * G4 * AUG, G4 * AUG), :].rearrange("(h p) n -> p h n", p=AUG)
            for r, (kq, kk) in enumerate((("qh", "kh"), ("qh", "kl"), ("ql", "kh"))):
                fetch(QS[i][r * HD:(r + 1) * HD, :, cols], src(kq))
                fetch(KS[i][r * HD:(r + 1) * HD, :, cols], src(kk))
            fetch(QS[i][3 * HD:ROWS, :, cols], norm("q"))
            fetch(KS[i][3 * HD:ROWS, :, cols], norm("k"))
            fetch(VS[i][:, half * TPB:(half + 1) * TPB, :],
                  v_d[ds(batch * N + half * HALF, HALF), ds(g * P, P)].rearrange("(j p) d -> p j d", p=P))

        STACK = 9 * 16
        STORES = 2 * 16

        class Attention:

            def __init__(self, m, i, before=None):
                self.m, self.i, self.sem, self.before = m, i, stage_sems[i], before

            def ticket(self, name, n):
                per = TILES if name in ("QK", "CL") else QUADS if name != "OZ" else QUADS // JC
                if n < 0:
                    return self.before.ticket(name, n + per) if self.before else None
                return self.sem[name], n + 1

            def tells(self, name, ins):
                ins.then_inc(self.sem[name], 1)

            def distances(self, t):
                q, pair = t // 2, t % 2
                gi, half, j = q // (2 * JC), q // JC % 2, q % JC
                wait(nc.tensor, self.ticket("CL", t - 2))
                if t == 0:
                    wait(nc.tensor, (stage_sems[1 - self.i]["stack0a"], STACK))
                if t == 2 * TPB:
                    wait(nc.tensor, (stage_sems[1 - self.i]["stack0b"], STACK))
                if t == TILES // 2:
                    wait(nc.tensor, (self.sem["stack1"], 2 * STACK))
                for h in (2 * pair, 2 * pair + 1):
                    col = (t % 2) * 2 * HALF + (h % 2) * HALF
                    mm = nc.tensor.matmul(pU[:, col:col + HALF], KS[gi][:, h, j * P:(j + 1) * P],
                                          QS[gi][:, h, half * HALF:(half + 1) * HALF], start=True, stop=True)
                self.tells("QK", mm)

            def clamp(self, t):
                q, pair = t // 2, t % 2
                wait(nc.vector, self.ticket("QK", t), self.ticket("WP", q - RING), self.ticket("WD", q - RING))
                cols = slice(pair * 2 * HALF, (pair + 1) * 2 * HALF)
                self.tells("CL", nc.vector.tensor_scalar(cosh[:, q % RING, cols], pU[:, cols], CS, None, ALU.max))

            def square(self, q):
                wait(nc.scalar, self.ticket("CL", 2 * q + 1), self.ticket("PV", q - RING))
                self.tells("SQ", nc.scalar.activation(root[:, q % RING, :], cosh[:, q % RING, :], ACT.Square))

            def sinh(self, q):
                wait(nc.scalar, self.ticket("SQ", q))
                self.tells("RT", nc.scalar.activation(root[:, q % RING, :], root[:, q % RING, :], ACT.Sqrt, bias=-CS * CS))

            def weights(self, name, engine, q, c):
                wait(engine, self.ticket("RT", q))
                self.tells(name, engine.tensor_tensor(root[:, q % RING, c], cosh[:, q % RING, c], root[:, q % RING, c], ALU.subtract))

            def sums(self, q):
                gi, half, j = q // (2 * JC), q // JC % 2, q % JC
                wait(nc.tensor, self.ticket("WP", q), self.ticket("WD", q))
                if j == 0:
                    wait(nc.tensor, self.ticket("OZ", q // JC - 1))
                for h in range(G4):
                    nc.tensor.matmul(pO[h * HD:(h + 1) * HD, :], VS[gi][:, j, h * HD:(h + 1) * HD],
                                     root[:, q % RING, h * HALF:(h + 1) * HALF], start=j == 0, stop=j == JC - 1)
                for h in range(G4):
                    mm = nc.tensor.matmul(pZ[h * HD:(h + 1) * HD, :], ones[:, :],
                                          root[:, q % RING, h * HALF:(h + 1) * HALF], start=j == 0, stop=j == JC - 1)
                self.tells("PV", mm)
                if j == JC - 1:
                    n = q // JC
                    wait(nc.scalar, self.ticket("PV", q), (self.sem["att"], n * STORES) if n else None)
                    nc.scalar.copy(o_s[:, :], pO[:, :])
                    self.tells("OZ", nc.scalar.copy(z_s[:, :], pZ[:, :]))
                    group = self.m * 2 + gi
                    batch, g = group // KC, group % KC
                    blk = batch * 2 + half
                    wait(nc.sync, self.ticket("OZ", n))
                    for dst, src in ((att_d[ds(blk * DM + g * P, P), :], o_s[:, :]), (z_d[ds(blk * H + g * G4, G4), :], z_s[0:P:HD, :])):
                        nc.sync.dma_start(dst, src).then_inc(self.sem["att"], 16)

            def stages(self, s):
                def run(stage, q):
                    body = self if q >= 0 else self.before
                    if body and body.m is not None:
                        stage(body, q % QUADS)

                if self.m is not None:
                    if s == 0:
                        self.distances(0)
                    if s + 1 < TILES:
                        self.distances(s + 1)
                    self.clamp(s)
                if s % 2:
                    run(Attention.sinh, s // 2 - 2)
                    run(lambda b, q: b.weights("WP", nc.gpsimd, q, slice(0, POOL_COLS)), s // 2 - 2)
                    run(lambda b, q: b.weights("WD", nc.vector, q, slice(POOL_COLS, G4 * HALF)), s // 2 - 3)
                else:
                    run(Attention.square, s // 2 - 1)
                    run(Attention.sums, s // 2 - 4)

        def finish_stages(last):
            use(1 - last.i)
            rest = Attention(None, 1 - last.i, last)
            for s in range(8):
                rest.stages(s)
            nc.sync.wait_ge(last.sem["att"], QUADS // JC * STORES)

        def attention(m, i, before, blk_in, blk_out, prefetch, fetched=True):
            use(i)
            mine, other = stage_sems[i], stage_sems[1 - i]
            body = Attention(m, i, before)
            misc, plan = Misc(), Schedule()
            if blk_in is not None:
                head, plan.units, _ = projections(blk_in, misc, (sets[1 - i]["x"].sem, 16), next_blk=(blk_in + 1) % NB)
                plan.at(HEAD, head)
            for s in range(TILES):
                body.stages(s)
                if s == HANDOVER:
                    for engine, names in ((nc.tensor, ("QK", "PV")), (nc.vector, ("CL", "WD")), (nc.scalar, ("SQ", "RT", "OZ")), (nc.gpsimd, ("WP",))):
                        if before:
                            for n in names:
                                engine.wait_ge(other[n], TILES if n in ("QK", "CL") else QUADS // JC if n == "OZ" else QUADS)
                        engine.sem_inc(mine["met"], 1)
                    nc.sync.wait_ge(mine["met"], 4)
                    if before:
                        nc.sync.wait_ge(other["att"], QUADS // JC * STORES)
                        nc.sync.wait_ge(other["stack1"], 2 * STACK)
                    if fetched:
                        nc.sync.wait_ge(sets[1 - i]["x"].sem, 16)
                    nc.sync.wait_ge(other["stack0a"], STACK)
                    nc.sync.wait_ge(other["stack0b"], STACK)
                    for sem in [*other.values(), *(sets[1 - i][n].sem for n in (*engines, *UNIT_TRANSFERS))]:
                        nc.sync.sem_clear(sem)
                    nc.sync.sem_inc(mine["clear"], 1)
                    if blk_out is not None:
                        head, tiles = output(blk_out, misc, buffers)
                        plan.at(HANDOVER + 2, head)
                        plan.units = merge(plan.units, tiles, OUT_FIRST, OUT_STEP)
                    for half in range(2):
                        load_stack(1, m * 2 + 1, half, mine["stack1"])
                if s == PREFETCH and prefetch:
                    wait(nc.sync, body.ticket("PV", QUADS // 2 - 1))
                    load_stack(0, m * 2 + 2, 0, mine["stack0a"])
                if s == CLEARED:
                    for engine in (nc.tensor, nc.vector, nc.scalar, nc.gpsimd):
                        engine.wait_ge(mine["clear"], 1)
                plan.issue(s, BUDGET[s % 2] if s > CLEARED else 0)
            plan.finish(TILES)
            for engine, name in zip((nc.tensor, nc.scalar, nc.vector, nc.gpsimd), engines):
                wait(engine, current_count(name))
            for name in transfers:
                if name != "x":
                    wait(nc.sync, current_count(name))
            if prefetch:
                load_stack(0, m * 2 + 2, 1, mine["stack0b"])
            return body

        def current_count(name):
            return (S[name].sem, S[name].count) if S[name].count else None

        def first_projections():
            misc, plan = Misc(), Schedule()
            head, units, before = projections(0, misc, tokens[0], xt)
            next_head, next_units, _ = projections(1, misc, tokens[1], xt1, before=before)
            plan.units = units + next_units
            plan.at(0, head)
            plan.at(FOLD, [(0, fold), (1, split_f), (4, split_o)])
            plan.at(NEXT_HEAD, next_head)
            plan.finish(0)
            meet()
            for k in "qkvof":
                weights[k] = None

        def outputs_only(first):
            misc, plan = Misc(), Schedule()
            views = lambda ring, i, j: ring[:, i, j * KC * 2 * P:(j + 1) * KC * 2 * P].rearrange("p (g n) -> p g n", g=KC)
            halves = root[:, 0, :].bitcast(F16)
            more = Buffers(cosh[:, 0, 0:2 * BLK * H // P].rearrange("p (s n) -> p s n", s=2), views(cosh, 1, 0), views(cosh, 1, 1),
                           halves[:, 0:KC * 2 * P].rearrange("p (g n) -> p g n", g=KC),
                           halves[:, KC * 2 * P:2 * KC * 2 * P].rearrange("p (g n) -> p g n", g=KC),
                           root[:, 1, 0:2 * DM].rearrange("p (s n) -> p s n", s=2))
            for k, (buf, which) in enumerate(((buffers, ""), (more, "+"))):
                head, tiles = output(first + k, misc, buf, which)
                plan.at(0, head)
                plan.units = merge(plan.units, tiles, 1, 2) if k else tiles
            plan.finish(0)
            meet()

        BODIES = B * KC // 2
        first_projections()
        load_stack(0, 0, 0, stage_sems[1]["stack0a"])
        load_stack(0, 0, 1, stage_sems[1]["stack0b"])

        nc.sync.dma_start(xt[:, :, :], x[LEAD * BLK:(LEAD + 1) * BLK, :].rearrange("(i p) n -> p i n", p=P)).then_inc(sets[1]["x"].sem, 16)

        even = Attention(0, 0)
        odd = Attention(0, 1)
        attention(0, 0, None, LEAD, None, True)
        even.m = 0
        attention(1, 1, even, 1 + LEAD, None, True)
        with nc.Fori(1, (BODIES - LEAD) // 2) as n:
            odd.m, even.m = n * 2 - 1, n * 2
            attention(n * 2, 0, odd, n * 2 + LEAD, n * 2 - LATE, True)
            attention(n * 2 + 1, 1, even, n * 2 + 1 + LEAD, n * 2 + 1 - LATE, True)
        odd.m, even.m = BODIES - 3, BODIES - 2
        attention(BODIES - 2, 0, odd, None, BODIES - 2 - LATE, True)
        odd.m = BODIES - 1
        attention(BODIES - 1, 1, even, None, BODIES - 1 - LATE, False, fetched=False)
        finish_stages(odd)
        use(0)
        meet()
        outputs_only(BODIES - LATE)


def general(nc, e):
    S, PE, AC, DV, PL = e["S"], e["PE"], e["AC"], e["DV"], e["PL"]
    meet, load, on_dve = e["meet"], e["load"], e["on_dve"]
    x, out, scale, v_d, res_d = e["x"], e["out"], e["scale"], e["v_d"], e["res_d"]
    IV = e["IV"]
    with ExitStack() as ctx:
        def sb(name, shape, dt=F32):
            return ctx.enter_context(nc.sbuf_tensor(name, shape, dt))

        q_t, k_t, o_t = (nc.dram_tensor(n, [DM, T], F32).ap() for n in ("q_t", "k_t", "o_t"))
        Wq, Wk, Wo = (sb(n, [P, KC, DM]) for n in ("Wq32", "Wk32", "Wo32"))
        idn, ones, two = sb("g_idn", [P, P]), sb("g_ones", [P, P]), sb("g_two", [P, 1])
        t0, t1, t2, t3, t4, t5 = (sb(f"t{i}", [P, DM]) for i in range(6))
        xn_t = sb("g_xn_t", [P, KC, P])
        stats, mv, small = sb("g_stats", [P, 6]), sb("g_mv", [P, 2]), sb("g_small", [P, 8])
        KF, QF = sb("KF", [96, N]), sb("QF", [96, N])
        Kh, sq = sb("Kh", [HD, N]), sb("sq", [HD, 2, N])
        Vh = sb("Vh", [P, JC, HD])
        a_b, b_p = sb("a_b", [P, N]), sb("b_p", [P, JC])
        o_sb = sb("o_sb", [HD, N])
        pA, pB, pC, pD, pE = (ctx.enter_context(nc.psum_tensor(f"g_p{n}", [P, HALF], F32)) for n in range(5))

        for dst, src in ((Wq, e["wq_t"]), (Wk, e["wk_t"]), (Wo, e["wo_t"])):
            load("load", dst[:, :, :], src.rearrange("(c p) n -> p c n", p=P))
        load("load", idn[:, :], e["ident"])
        DV.done(nc.vector.memset(ones[:, :], 1.0))
        DV.done(nc.vector.memset(two[:, :], 2.0))
        DV.done(nc.vector.memset(KF[:, :], 0.0))
        on_dve(nc.vector.memset(QF[:, :], 0.0))
        DV.done(nc.vector.memset(KF[32:33, :], 1.0))
        DV.done(nc.vector.memset(QF[64:65, :], 1.0))
        meet()

        with nc.Fori(0, NT) as n:
            row = n * P
            wait(nc.vector, load("x", t0[:, :], x[ds(row, P), :]))
            on_dve(nc.vector.bn_stats(stats[:, :], t0[:, :]))
            on_dve(nc.vector.bn_aggr(mv[:, :], stats[:, :]))
            r = DV.done(nc.vector.tensor_scalar(small[:, 0:1], mv[:, 1:2], EPS, None, ALU.add))
            wait(nc.scalar, r)
            r = AC.done(nc.scalar.activation(small[:, 1:2], small[:, 0:1], ACT.Sqrt))
            wait(nc.vector, r)
            on_dve(nc.vector.reciprocal(small[:, 2:3], small[:, 1:2]))
            on_dve(nc.vector.tensor_scalar(small[:, 3:4], small[:, 0:1], small[:, 2:3], small[:, 2:3], ALU.mult, ALU.mult))
            on_dve(nc.vector.tensor_scalar(small[:, 4:5], small[:, 3:4], -0.5, 1.5, ALU.mult, ALU.add))
            on_dve(nc.vector.tensor_scalar(small[:, 5:6], small[:, 4:5], small[:, 2:3], None, ALU.mult))
            xn = DV.done(nc.vector.tensor_scalar(t1[:, :], t0[:, :], mv[:, 0:1], small[:, 5:6], ALU.subtract, ALU.mult))
            wait(nc.tensor, xn)
            for c in range(KC):
                m = nc.tensor.transpose(pA[:, c * P:(c + 1) * P], t1[:, c * P:(c + 1) * P], idn[:, :])
            wait(nc.vector, PE.done(m))
            xt = DV.done(nc.vector.tensor_copy(xn_t[:, :, :], pA[:, :].rearrange("p (c n) -> p c n", c=KC)))
            wait(nc.tensor, xt)
            for psum, W, hold, dst in ((pB, Wq, t3, q_t), (pC, Wk, t4, k_t)):
                for o in range(KC):
                    for c in range(KC):
                        m = nc.tensor.matmul(psum[:, o * P:(o + 1) * P], W[:, c, o * P:(o + 1) * P], xn_t[:, c, :],
                                             start=c == 0, stop=c == KC - 1)
                wait(nc.vector, PE.done(m))
                r = DV.done(nc.vector.tensor_copy(hold[:, :], psum[:, :]))
                wait(nc.sync, r)
                load("out0", dst.rearrange("(c p) n -> p c n", p=P)[:, :, ds(row, P)],
                     hold[:, :].rearrange("p (c n) -> p c n", c=KC))
            meet()

        with nc.Fori(0, B) as bi:
            with nc.Fori(0, H) as h:
                col, feat = bi * N, h * HD
                load("load", Kh[:, :], k_t[ds(feat, HD), ds(col, N)])
                load("load", QF[0:HD, :], q_t[ds(feat, HD), ds(col, N)])
                ld = load("load", Vh[:, :, :], v_d[ds(col, N), ds(feat, HD)].rearrange("(j p) d -> p j d", p=P))
                wait(nc.vector, ld)
                DV.done(nc.vector.tensor_scalar(KF[0:HD, :], Kh[:, :], -2.0, None, ALU.mult))
                DV.done(nc.vector.tensor_tensor(sq[:, 0, :], Kh[:, :], Kh[:, :], ALU.mult))
                s = DV.done(nc.vector.tensor_tensor(sq[:, 1, :], QF[0:HD, :], QF[0:HD, :], ALU.mult))
                wait(nc.tensor, s)
                for i in range(2):
                    cols = slice(i * HALF, (i + 1) * HALF)
                    nc.tensor.matmul(pA[32:64, :], ones[0:HD, 0:32], sq[:, 1, cols], start=True, stop=True)
                    nc.tensor.matmul(pA[64:96, :], ones[0:HD, 0:32], sq[:, 0, cols], start=True, stop=True)
                    m = PE.done(nc.tensor.matmul(pB[:, :], ones[0:HD, :], sq[:, 1, cols], start=True, stop=True))
                    wait(nc.vector, m)
                    DV.done(nc.vector.tensor_copy(QF[32:33, cols], pA[32:33, :]))
                    DV.done(nc.vector.tensor_copy(KF[64:65, cols], pA[64:65, :]))
                    s = DV.done(nc.vector.tensor_scalar(a_b[:, cols], pB[:, :], -1.0, 1.0, ALU.mult, ALU.add))
                    wait(nc.tensor, s)
                for j in range(JC):
                    m = nc.tensor.matmul(pC[:, j:j + 1], sq[:, 0, j * P:(j + 1) * P], ones[0:HD, 0:1], start=True, stop=True)
                wait(nc.vector, PE.done(m))
                on_dve(nc.vector.tensor_scalar(b_p[:, :], pC[:, 0:JC], -1.0, 1.0, ALU.mult, ALU.add))
                for i in range(2):
                    cols = slice(i * HALF, (i + 1) * HALF)
                    for j in range(JC):
                        m = PE.done(nc.tensor.matmul(pA[:, :], KF[:, j * P:(j + 1) * P], QF[:, cols], start=True, stop=True))
                        on_dve(nc.vector.tensor_scalar(t0[:, :], a_b[:, cols], b_p[:, j:j + 1], 1e-6, ALU.mult, ALU.max))
                        on_dve(nc.vector.reciprocal(t1[:, :], t0[:, :]))
                        wait(nc.vector, m)
                        u = DV.done(nc.vector.scalar_tensor_tensor(out=t2[:, :], in0=pA[:, :], scalar=0.0, in1=t1[:, :], op0=ALU.max, op1=ALU.mult))
                        wait(nc.scalar, u)
                        AC.done(nc.scalar.activation(t3[:, :], t2[:, :], ACT.Sqrt, scale=2.0))
                        s = AC.done(nc.scalar.activation(t4[:, :], t2[:, :], ACT.Sqrt, scale=2.0, bias=two[:, 0:1]))
                        wait(nc.vector, s)
                        on_dve(nc.vector.tensor_tensor(t5[:, :], t3[:, :], t4[:, :], ALU.mult))
                        on_dve(nc.vector.scalar_tensor_tensor(out=t0[:, :], in0=t2[:, :], scalar=2.0, in1=t5[:, :], op0=ALU.mult, op1=ALU.add))
                        on_dve(nc.vector.tensor_scalar(t1[:, :], t0[:, :], 1.0, None, ALU.add))
                        w = DV.done(nc.vector.reciprocal(t0[:, :], t1[:, :]))
                        wait(nc.tensor, w)
                        nc.tensor.matmul(pD[0:HD, :], Vh[:, j, :], t0[:, :], start=j == 0, stop=j == JC - 1)
                        m = PE.done(nc.tensor.matmul(pE[0:HD, :], ones[:, 0:HD], t0[:, :], start=j == 0, stop=j == JC - 1))
                        wait(nc.vector, m)
                    on_dve(nc.vector.reciprocal(t1[0:HD, :], pE[0:HD, :]))
                    s = on_dve(nc.vector.tensor_tensor(o_sb[:, cols], pD[0:HD, :], t1[0:HD, :], ALU.mult))
                    wait(nc.tensor, s)
                wait(nc.sync, s)
                load("out0", o_t[ds(feat, HD), ds(col, N)], o_sb[:, :])
                meet()

        with nc.Fori(0, NT) as n:
            row = n * P
            load("load", xn_t[:, :, :], o_t.rearrange("(c p) n -> p c n", p=P)[:, :, ds(row, P)])
            ld = load("load", t0[:, :], res_d[ds(row, P), :])
            wait(nc.tensor, ld)
            for c in range(KC):
                m = nc.tensor.matmul(pA[:, :], xn_t[:, c, :], Wo[:, c, :], start=c == 0, stop=c == KC - 1)
            wait(nc.vector, PE.done(m), ld)
            s = DV.done(nc.vector.scalar_tensor_tensor(out=t1[:, :], in0=pA[:, :], scalar=scale[:, IV:IV + 1], in1=t0[:, :],
                                                       op0=ALU.mult, op1=ALU.add))
            wait(nc.sync, s)
            load("out0", out[ds(row, P), :], t1[:, :])
            meet()


def kernel(L0_attn_x, L0_attn_Wq, L0_attn_Wk, L0_attn_Wv, L0_attn_Wo, L0_ffn_kernel, L0_ffn_bias, L0_ffn_a, L0_ffn_b):
    import numpy as np
    import concourse.bacc as bacc
    from concourse.bass_utils import run_bass_kernel_spmd

    lay = np.ascontiguousarray
    arrays = {
        "x": lay(np.asarray(L0_attn_x).reshape(T, DM)),
        "wq_t": lay(np.asarray(L0_attn_Wq).T), "wk_t": lay(np.asarray(L0_attn_Wk).T),
        "wv_t": lay(np.asarray(L0_attn_Wv).T), "wo_t": lay(np.asarray(L0_attn_Wo).T),
        "ffn_w": lay(L0_ffn_kernel),
        "bias": lay(np.broadcast_to(np.asarray(L0_ffn_bias), (P, DM))),
        "a_t": lay(np.asarray(L0_ffn_a).T), "b": lay(L0_ffn_b),
        "ident": np.eye(P, dtype=np.float32),
    }
    nc = bacc.Bacc("TRN2", target_bir_lowering=False, num_devices=1)
    args = {k: nc.dram_tensor(f"in_{k}", a.shape, F32, kind="ExternalInput").ap() for k, a in arrays.items()}
    out = nc.dram_tensor("out_0", (T, DM), F32, kind="ExternalOutput").ap()
    build(nc, out=out, **args)
    r = run_bass_kernel_spmd(nc, [{f"in_{k}": a for k, a in arrays.items()}], core_ids=[0])
    return r.results[0]["out_0"].reshape(B, N, DM)
```
